# Optimizing a Trainium2 kernel written in Bass

```python
import numpy as np
import jax
import jax.numpy as jnp

def _softmax(x, axis=-1):
    return jax.nn.softmax(x, axis=axis)

def _gelu(x):
    return jax.nn.gelu(x, approximate=True)

def _silu(x):
    return jax.nn.silu(x)

def _sigmoid(x):
    return jax.nn.sigmoid(x)

def _layernorm(x, axis=-1, eps=1e-05):
    m = jnp.mean(x, axis=axis, keepdims=True)
    v = jnp.var(x, axis=axis, keepdims=True)
    return (x - m) / jnp.sqrt(v + eps)

def _scatter_add(tgt, idx, src, axis=0):
    return tgt.at[idx].add(src)

def _segment_sum(src, seg, n):
    return jax.ops.segment_sum(src, seg, n)
kernel_name = 'mk_xattn_ffn_d2_seqx_r8_478498'

def setup_inputs(seed: int=0):
    np.random.seed(seed)
    _w = jnp.asarray

    def _rec_inputs():
        import jax
        import jax.numpy as jnp
        _rk = jax.random.key(seed)
        x = -0.0002928 + 1 * jax.random.normal(jax.random.fold_in(_rk, 1), (64, 128, 128), jnp.float32)
        _lenS = 128 - jax.random.randint(jax.random.fold_in(_rk, 7), (64,), 0, max(1, 128 // 4) + 1, jnp.int32)
        _lenS2 = 120 - jax.random.randint(jax.random.fold_in(_rk, 8), (64,), 0, max(1, 120 // 4) + 1, jnp.int32)
        _ctx_512P = jax.random.normal(jax.random.fold_in(_rk, 11), (64, 16, 64), jnp.float32)
        _ctx_512c = jax.random.dirichlet(jax.random.fold_in(_rk, 511), 0.3 * jnp.ones((16,), jnp.float32), (64, 120))
        _ctx_512t = jnp.einsum('bsk,bkd->bsd', _ctx_512c, _ctx_512P)
        _ctx_512t = _ctx_512t * jax.lax.rsqrt(jnp.mean(jnp.square(_ctx_512t)) + 1e-12) * 0.953939
        ctx_512 = -0.000514642 + 1.00011 * (_ctx_512t + 0.3 * jax.random.normal(jax.random.fold_in(_rk, 611), (64, 120, 64), jnp.float32))
        return (x, ctx_512)
    x, ctx_512 = _rec_inputs()

    def _L0_xattn_setup():
        import jax, jax.numpy as jnp
        import numpy as np
        DIM = 128
        LATENT_DIM = 64
        NUM_HEADS = 16
        HEAD_DIM = DIM // NUM_HEADS
        SCALE = HEAD_DIM ** (-0.5)
        key = jax.random.key(seed)
        k1, k2, k3, k4, k5 = jax.random.split(key, 5)
        B, xN, zN = (2, 256, 256)
        x = jax.random.normal(k1, (B, xN, DIM), dtype=jnp.float32)
        z = jax.random.normal(k2, (B, zN, LATENT_DIM), dtype=jnp.float32)
        Wq = jax.random.normal(k3, (DIM, DIM), dtype=jnp.float32) * DIM ** (-0.5)
        Wkv = jax.random.normal(k4, (2 * DIM, LATENT_DIM), dtype=jnp.float32) * LATENT_DIM ** (-0.5)
        Wo = jax.random.normal(k5, (DIM, DIM), dtype=jnp.float32) * DIM ** (-0.5)
        return {'x': x, 'z': z, 'Wq': Wq, 'Wkv': Wkv, 'Wo': Wo}
    _L0_xattn_all = _L0_xattn_setup()
    _L0_xattn_in = {k: v for k, v in _L0_xattn_all.items() if k in ('Wq', 'Wkv', 'Wo')}
    del _L0_xattn_all

    def _L0_ffn_setup():
        import jax, jax.numpy as jnp
        import numpy as np
        D_MODEL, D_FF, N_EXP = (128, 512, 8)
        key = jax.random.key(seed)
        ks = jax.random.split(key, 8)
        s = lambda fan_in: 1.0 / np.sqrt(fan_in)
        x = jax.random.normal(ks[0], (4, 256, D_MODEL), dtype=jnp.float32)
        Wr = jax.random.uniform(ks[1], (N_EXP, D_MODEL), jnp.float32, -s(D_MODEL), s(D_MODEL))
        br = jax.random.uniform(ks[2], (N_EXP,), jnp.float32, -s(D_MODEL), s(D_MODEL))
        W1 = jax.random.uniform(ks[3], (N_EXP, D_FF, D_MODEL), jnp.float32, -s(D_MODEL), s(D_MODEL))
        b1 = jax.random.uniform(ks[4], (N_EXP, D_FF), jnp.float32, -s(D_MODEL), s(D_MODEL))
        W2 = jax.random.uniform(ks[5], (N_EXP, D_MODEL, D_FF), jnp.float32, -s(D_FF), s(D_FF))
        b2 = jax.random.uniform(ks[6], (N_EXP, D_MODEL), jnp.float32, -s(D_FF), s(D_FF))
        return {'x': x, 'Wr': Wr, 'br': br, 'W1': W1, 'b1': b1, 'W2': W2, 'b2': b2}
    _L0_ffn_all = _L0_ffn_setup()
    _L0_ffn_in = {k: v for k, v in _L0_ffn_all.items() if k in ('Wr', 'br', 'W1', 'b1', 'W2', 'b2')}
    del _L0_ffn_all

    def _L1_xattn_setup():
        import jax, jax.numpy as jnp
        import numpy as np
        H, D, C1, C2, S, M, B, W = (16, 32, 128, 64, 256, 64, 2, 4)

        def _ln(x, g, b):
            m = jnp.mean(x, -1, keepdims=True)
            v = jnp.var(x, -1, keepdims=True)
            return (x - m) * jax.lax.rsqrt(v + 1e-05) * g + b

        def _mha(x, y, wq, wk, wv, li1_w, li1_b, lnx_g, lnx_b, lny_g, lny_b, ln3_g, ln3_b, li2_w, li2_b, li3_w, li3_b, causal):
            xn = _ln(x, lnx_g, lnx_b)
            yn = _ln(y, lny_g, lny_b)
            q = jnp.einsum('bsc,hcd->bhsd', xn, wq)
            k = jnp.einsum('btc,hcd->bhtd', yn, wk)
            v = jnp.einsum('btc,hcd->bhtd', yn, wv)
            a = jax.nn.softmax(jnp.einsum('bhsd,bhtd->bhst', q, k) * D ** (-0.5), axis=-1)
            if causal:
                s, t = (a.shape[-2], a.shape[-1])
                mask = (jnp.arange(t)[None, :] > jnp.arange(s)[:, None]).astype(a.dtype)
                a = a * mask
            o = jnp.einsum('bhst,bhtd->bhsd', a, v)
            o = o.transpose(0, 2, 1, 3).reshape(x.shape[0], x.shape[1], H * D)
            x_out = x + o @ li1_w + li1_b
            h = jax.nn.gelu(_ln(x_out, ln3_g, ln3_b) @ li2_w + li2_b, approximate=False)
            return x_out + h @ li3_w + li3_b
        key = jax.random.key(seed)
        ks = iter(jax.random.split(key, 64))

        def w(shape, scale=0.02):
            return jax.random.normal(next(ks), shape, jnp.float32) * scale
        inp = {'xx': jax.random.normal(next(ks), (B, S, C1), jnp.float32), 'ee': jax.random.normal(next(ks), (B, M, C2), jnp.float32), 'ln1_g': jnp.ones(C1, jnp.float32), 'ln1_b': jnp.zeros(C1, jnp.float32), 'ln2_g': jnp.ones(C1, jnp.float32), 'ln2_b': jnp.zeros(C1, jnp.float32)}
        for pfx, cy in (('a1', C1), ('a2', C2)):
            inp[pfx + '_wq'] = w((H, C1, D))
            inp[pfx + '_wk'] = w((H, cy, D))
            inp[pfx + '_wv'] = w((H, cy, D))
            inp[pfx + '_li1_w'] = w((H * D, C1))
            inp[pfx + '_li1_b'] = jnp.zeros(C1, jnp.float32)
            inp[pfx + '_lnx_g'] = jnp.ones(C1, jnp.float32)
            inp[pfx + '_lnx_b'] = jnp.zeros(C1, jnp.float32)
            inp[pfx + '_lny_g'] = jnp.ones(cy, jnp.float32)
            inp[pfx + '_lny_b'] = jnp.zeros(cy, jnp.float32)
            inp[pfx + '_ln3_g'] = jnp.ones(C1, jnp.float32)
            inp[pfx + '_ln3_b'] = jnp.zeros(C1, jnp.float32)
            inp[pfx + '_li2_w'] = w((C1, C1 * W))
            inp[pfx + '_li2_b'] = jnp.zeros(C1 * W, jnp.float32)
            inp[pfx + '_li3_w'] = w((C1 * W, C1))
            inp[pfx + '_li3_b'] = jnp.zeros(C1, jnp.float32)
        inp['training'] = 0
        return inp
    _L1_xattn_all = _L1_xattn_setup()
    _L1_xattn_in = {k: v for k, v in _L1_xattn_all.items() if k in ('ln1_g', 'ln1_b', 'ln2_g', 'ln2_b', 'a1_wq', 'a1_wk', 'a1_wv', 'a1_li1_w', 'a1_li1_b', 'a1_lnx_g', 'a1_lnx_b', 'a1_lny_g', 'a1_lny_b', 'a1_ln3_g', 'a1_ln3_b', 'a1_li2_w', 'a1_li2_b', 'a1_li3_w', 'a1_li3_b', 'a2_wq', 'a2_wk', 'a2_wv', 'a2_li1_w', 'a2_li1_b', 'a2_lnx_g', 'a2_lnx_b', 'a2_lny_g', 'a2_lny_b', 'a2_ln3_g', 'a2_ln3_b', 'a2_li2_w', 'a2_li2_b', 'a2_li3_w', 'a2_li3_b')}
    del _L1_xattn_all

    def _L1_ffn_setup():
        import jax, jax.numpy as jnp
        import numpy as np
        S, B, H = (256, 4, 128)
        E = 64
        K = 4
        I = 64
        CAP = 128
        key = jax.random.key(seed)
        k1, k2, k3, k4 = jax.random.split(key, 4)
        return {'hidden_states': jax.random.normal(k1, (S, B, H), dtype=jnp.float32), 'router_w': jax.random.normal(k2, (H, E), dtype=jnp.float32) * 0.02, 'w1': jax.random.normal(k3, (E, H, 2 * I), dtype=jnp.float32) * 0.02, 'w2': jax.random.normal(k4, (E, I, H), dtype=jnp.float32) * 0.02}
    _L1_ffn_all = _L1_ffn_setup()
    _L1_ffn_in = {k: v for k, v in _L1_ffn_all.items() if k in ('router_w', 'w1', 'w2')}
    del _L1_ffn_all
    return {'x': x, 'ctx_512': ctx_512, 'L0_xattn_Wq': _L0_xattn_in['Wq'], 'L0_xattn_Wkv': _L0_xattn_in['Wkv'], 'L0_xattn_Wo': _L0_xattn_in['Wo'], 'L0_ffn_Wr': _L0_ffn_in['Wr'], 'L0_ffn_br': _L0_ffn_in['br'], 'L0_ffn_W1': _L0_ffn_in['W1'], 'L0_ffn_b1': _L0_ffn_in['b1'], 'L0_ffn_W2': _L0_ffn_in['W2'], 'L0_ffn_b2': _L0_ffn_in['b2'], 'L1_xattn_ln1_g': _L1_xattn_in['ln1_g'], 'L1_xattn_ln1_b': _L1_xattn_in['ln1_b'], 'L1_xattn_ln2_g': _L1_xattn_in['ln2_g'], 'L1_xattn_ln2_b': _L1_xattn_in['ln2_b'], 'L1_xattn_a1_wq': _L1_xattn_in['a1_wq'], 'L1_xattn_a1_wk': _L1_xattn_in['a1_wk'], 'L1_xattn_a1_wv': _L1_xattn_in['a1_wv'], 'L1_xattn_a1_li1_w': _L1_xattn_in['a1_li1_w'], 'L1_xattn_a1_li1_b': _L1_xattn_in['a1_li1_b'], 'L1_xattn_a1_lnx_g': _L1_xattn_in['a1_lnx_g'], 'L1_xattn_a1_lnx_b': _L1_xattn_in['a1_lnx_b'], 'L1_xattn_a1_lny_g': _L1_xattn_in['a1_lny_g'], 'L1_xattn_a1_lny_b': _L1_xattn_in['a1_lny_b'], 'L1_xattn_a1_ln3_g': _L1_xattn_in['a1_ln3_g'], 'L1_xattn_a1_ln3_b': _L1_xattn_in['a1_ln3_b'], 'L1_xattn_a1_li2_w': _L1_xattn_in['a1_li2_w'], 'L1_xattn_a1_li2_b': _L1_xattn_in['a1_li2_b'], 'L1_xattn_a1_li3_w': _L1_xattn_in['a1_li3_w'], 'L1_xattn_a1_li3_b': _L1_xattn_in['a1_li3_b'], 'L1_xattn_a2_wq': _L1_xattn_in['a2_wq'], 'L1_xattn_a2_wk': _L1_xattn_in['a2_wk'], 'L1_xattn_a2_wv': _L1_xattn_in['a2_wv'], 'L1_xattn_a2_li1_w': _L1_xattn_in['a2_li1_w'], 'L1_xattn_a2_li1_b': _L1_xattn_in['a2_li1_b'], 'L1_xattn_a2_lnx_g': _L1_xattn_in['a2_lnx_g'], 'L1_xattn_a2_lnx_b': _L1_xattn_in['a2_lnx_b'], 'L1_xattn_a2_lny_g': _L1_xattn_in['a2_lny_g'], 'L1_xattn_a2_lny_b': _L1_xattn_in['a2_lny_b'], 'L1_xattn_a2_ln3_g': _L1_xattn_in['a2_ln3_g'], 'L1_xattn_a2_ln3_b': _L1_xattn_in['a2_ln3_b'], 'L1_xattn_a2_li2_w': _L1_xattn_in['a2_li2_w'], 'L1_xattn_a2_li2_b': _L1_xattn_in['a2_li2_b'], 'L1_xattn_a2_li3_w': _L1_xattn_in['a2_li3_w'], 'L1_xattn_a2_li3_b': _L1_xattn_in['a2_li3_b'], 'L1_ffn_router_w': _L1_ffn_in['router_w'], 'L1_ffn_w1': _L1_ffn_in['w1'], 'L1_ffn_w2': _L1_ffn_in['w2']}

def reference(x, ctx_512, L0_xattn_Wq, L0_xattn_Wkv, L0_xattn_Wo, L0_ffn_Wr, L0_ffn_br, L0_ffn_W1, L0_ffn_b1, L0_ffn_W2, L0_ffn_b2, L1_xattn_ln1_g, L1_xattn_ln1_b, L1_xattn_ln2_g, L1_xattn_ln2_b, L1_xattn_a1_wq, L1_xattn_a1_wk, L1_xattn_a1_wv, L1_xattn_a1_li1_w, L1_xattn_a1_li1_b, L1_xattn_a1_lnx_g, L1_xattn_a1_lnx_b, L1_xattn_a1_lny_g, L1_xattn_a1_lny_b, L1_xattn_a1_ln3_g, L1_xattn_a1_ln3_b, L1_xattn_a1_li2_w, L1_xattn_a1_li2_b, L1_xattn_a1_li3_w, L1_xattn_a1_li3_b, L1_xattn_a2_wq, L1_xattn_a2_wk, L1_xattn_a2_wv, L1_xattn_a2_li1_w, L1_xattn_a2_li1_b, L1_xattn_a2_lnx_g, L1_xattn_a2_lnx_b, L1_xattn_a2_lny_g, L1_xattn_a2_lny_b, L1_xattn_a2_ln3_g, L1_xattn_a2_ln3_b, L1_xattn_a2_li2_w, L1_xattn_a2_li2_b, L1_xattn_a2_li3_w, L1_xattn_a2_li3_b, L1_ffn_router_w, L1_ffn_w1, L1_ffn_w2):
    import jax
    import jax.numpy as jnp

    def _L0_xattn_ref(x, z, Wq, Wkv, Wo):
        import jax, jax.numpy as jnp
        import numpy as np
        DIM = 128
        LATENT_DIM = 64
        NUM_HEADS = 16
        HEAD_DIM = DIM // NUM_HEADS
        SCALE = HEAD_DIM ** (-0.5)
        B, xN, _ = x.shape
        _, zN, _ = z.shape
        Q = (x @ Wq.T).reshape(B, xN, NUM_HEADS, HEAD_DIM)
        KV = (z @ Wkv.T).reshape(B, zN, 2, NUM_HEADS, HEAD_DIM)
        K = KV[:, :, 0]
        V = KV[:, :, 1]
        attn = jnp.einsum('bqhd,bkhd->bhqk', Q, K) * SCALE
        attn = jax.nn.softmax(attn, axis=-1)
        O = jnp.einsum('bhqk,bkhd->bqhd', attn, V).reshape(B, xN, DIM)
        return O @ Wo.T

    def _L0_ffn_ref(x, Wr, br, W1, b1, W2, b2):
        import jax, jax.numpy as jnp
        import numpy as np
        D_MODEL, D_FF, N_EXP = (128, 512, 8)
        B, S, D = x.shape
        xf = x.reshape(-1, D)
        logits = xf @ Wr.T + br
        expert_idx = jnp.argmax(logits, axis=-1)
        h = jax.nn.relu(jnp.einsum('td,efd->etf', xf, W1) + b1[:, None, :])
        y = jnp.einsum('etf,edf->etd', h, W2) + b2[:, None, :]
        out = y[expert_idx, jnp.arange(xf.shape[0])]
        return out.reshape(B, S, D)

    def _L1_xattn_ref(xx, ee, ln1_g, ln1_b, ln2_g, ln2_b, a1_wq, a1_wk, a1_wv, a1_li1_w, a1_li1_b, a1_lnx_g, a1_lnx_b, a1_lny_g, a1_lny_b, a1_ln3_g, a1_ln3_b, a1_li2_w, a1_li2_b, a1_li3_w, a1_li3_b, a2_wq, a2_wk, a2_wv, a2_li1_w, a2_li1_b, a2_lnx_g, a2_lnx_b, a2_lny_g, a2_lny_b, a2_ln3_g, a2_ln3_b, a2_li2_w, a2_li2_b, a2_li3_w, a2_li3_b, training):
        import jax, jax.numpy as jnp
        import numpy as np
        H, D, C1, C2, S, M, B, W = (16, 32, 128, 64, 256, 64, 2, 4)

        def _ln(x, g, b):
            m = jnp.mean(x, -1, keepdims=True)
            v = jnp.var(x, -1, keepdims=True)
            return (x - m) * jax.lax.rsqrt(v + 1e-05) * g + b

        def _mha(x, y, wq, wk, wv, li1_w, li1_b, lnx_g, lnx_b, lny_g, lny_b, ln3_g, ln3_b, li2_w, li2_b, li3_w, li3_b, causal):
            xn = _ln(x, lnx_g, lnx_b)
            yn = _ln(y, lny_g, lny_b)
            q = jnp.einsum('bsc,hcd->bhsd', xn, wq)
            k = jnp.einsum('btc,hcd->bhtd', yn, wk)
            v = jnp.einsum('btc,hcd->bhtd', yn, wv)
            a = jax.nn.softmax(jnp.einsum('bhsd,bhtd->bhst', q, k) * D ** (-0.5), axis=-1)
            if causal:
                s, t = (a.shape[-2], a.shape[-1])
                mask = (jnp.arange(t)[None, :] > jnp.arange(s)[:, None]).astype(a.dtype)
                a = a * mask
            o = jnp.einsum('bhst,bhtd->bhsd', a, v)
            o = o.transpose(0, 2, 1, 3).reshape(x.shape[0], x.shape[1], H * D)
            x_out = x + o @ li1_w + li1_b
            h = jax.nn.gelu(_ln(x_out, ln3_g, ln3_b) @ li2_w + li2_b, approximate=False)
            return x_out + h @ li3_w + li3_b
        x = _ln(xx, ln1_g, ln1_b)
        x = x + _mha(x, x, a1_wq, a1_wk, a1_wv, a1_li1_w, a1_li1_b, a1_lnx_g, a1_lnx_b, a1_lny_g, a1_lny_b, a1_ln3_g, a1_ln3_b, a1_li2_w, a1_li2_b, a1_li3_w, a1_li3_b, causal=True)
        x = _ln(x, ln2_g, ln2_b)
        return x + _mha(x, ee, a2_wq, a2_wk, a2_wv, a2_li1_w, a2_li1_b, a2_lnx_g, a2_lnx_b, a2_lny_g, a2_lny_b, a2_ln3_g, a2_ln3_b, a2_li2_w, a2_li2_b, a2_li3_w, a2_li3_b, causal=False)

    def _L1_ffn_ref(hidden_states, router_w, w1, w2):
        import jax, jax.numpy as jnp
        import numpy as np
        S, B, H = (256, 4, 128)
        E = 64
        K = 4
        I = 64
        CAP = 128
        s, b, h = hidden_states.shape
        x = hidden_states.reshape(-1, h)
        T = x.shape[0]
        P = T * K
        logits = x @ router_w
        probs_all = jax.nn.softmax(logits, axis=-1)
        top_p, top_i = jax.lax.top_k(probs_all, K)
        rows = jnp.arange(T)[:, None]
        routing_map = jnp.zeros((T, E), dtype=bool).at[rows, top_i].set(True)
        probs = jnp.zeros((T, E), dtype=x.dtype).at[rows, top_i].set(top_p)
        flat = routing_map.T.reshape(-1)
        order = jnp.argsort((~flat).astype(jnp.int32), stable=True)[:P]
        expert_id = order // T
        token_idx = order % T
        group_sizes = routing_map.sum(axis=0)
        starts = jnp.cumsum(group_sizes) - group_sizes
        pos = jnp.arange(P) - starts[expert_id]
        perm_x = x[token_idx]
        buf = jnp.zeros((E, CAP, h), dtype=x.dtype).at[expert_id, pos].set(perm_x)
        h1 = jnp.einsum('ech,ehf->ecf', buf, w1)
        g = jax.nn.silu(h1[..., :I]) * h1[..., I:]
        y = jnp.einsum('eci,eih->ech', g, w2)
        perm_y = y[expert_id, pos]
        perm_probs = probs.T.reshape(-1)[order]
        out = jnp.zeros((T, h), dtype=x.dtype).at[token_idx].add(perm_y * perm_probs[:, None])
        return out.reshape(s, b, h)
    x = x + _L0_xattn_ref(_layernorm(x, axis=-1), ctx_512, L0_xattn_Wq, L0_xattn_Wkv, L0_xattn_Wo)
    x = x + _L0_ffn_ref(_layernorm(x, axis=-1), L0_ffn_Wr, L0_ffn_br, L0_ffn_W1, L0_ffn_b1, L0_ffn_W2, L0_ffn_b2)
    x = x + _L1_xattn_ref(_layernorm(x, axis=-1), ctx_512, L1_xattn_ln1_g, L1_xattn_ln1_b, L1_xattn_ln2_g, L1_xattn_ln2_b, L1_xattn_a1_wq, L1_xattn_a1_wk, L1_xattn_a1_wv, L1_xattn_a1_li1_w, L1_xattn_a1_li1_b, L1_xattn_a1_lnx_g, L1_xattn_a1_lnx_b, L1_xattn_a1_lny_g, L1_xattn_a1_lny_b, L1_xattn_a1_ln3_g, L1_xattn_a1_ln3_b, L1_xattn_a1_li2_w, L1_xattn_a1_li2_b, L1_xattn_a1_li3_w, L1_xattn_a1_li3_b, L1_xattn_a2_wq, L1_xattn_a2_wk, L1_xattn_a2_wv, L1_xattn_a2_li1_w, L1_xattn_a2_li1_b, L1_xattn_a2_lnx_g, L1_xattn_a2_lnx_b, L1_xattn_a2_lny_g, L1_xattn_a2_lny_b, L1_xattn_a2_ln3_g, L1_xattn_a2_ln3_b, L1_xattn_a2_li2_w, L1_xattn_a2_li2_b, L1_xattn_a2_li3_w, L1_xattn_a2_li3_b, 0)
    x = x + _L1_ffn_ref(_layernorm(x, axis=-1), L1_ffn_router_w, L1_ffn_w1, L1_ffn_w2)
    return x

_drawn_inputs = setup_inputs


def setup_inputs(seed=0):
    import zlib

    import numpy as np

    out = dict(_drawn_inputs(seed))
    spreads = {'L1_xattn_ln1_g': (1.0, 0.2),
     'L1_xattn_ln1_b': (0.0, 0.1),
     'L1_xattn_ln2_g': (1.0, 0.2),
     'L1_xattn_ln2_b': (0.0, 0.1),
     'L1_xattn_a1_li1_b': (0.0, 0.268),
     'L1_xattn_a1_lnx_g': (1.0, 0.6),
     'L1_xattn_a1_lnx_b': (0.0, 0.8),
     'L1_xattn_a1_lny_g': (1.0, 0.6),
     'L1_xattn_a1_lny_b': (0.0, 0.8),
     'L1_xattn_a1_ln3_g': (1.0, 0.6),
     'L1_xattn_a1_ln3_b': (0.0, 0.8),
     'L1_xattn_a1_li2_b': (0.0, 0.8),
     'L1_xattn_a1_li3_b': (0.0, 0.1),
     'L1_xattn_a2_li1_b': (0.0, 0.28),
     'L1_xattn_a2_lnx_g': (1.0, 0.6),
     'L1_xattn_a2_lnx_b': (0.0, 0.8),
     'L1_xattn_a2_lny_g': (1.0, 0.6),
     'L1_xattn_a2_lny_b': (0.0, 0.8),
     'L1_xattn_a2_ln3_g': (1.0, 0.6),
     'L1_xattn_a2_ln3_b': (0.0, 0.8),
     'L1_xattn_a2_li2_b': (0.0, 0.8),
     'L1_xattn_a2_li3_b': (0.0, 0.1)}
    factors = {'L0_ffn_b1': 3.271,
     'L1_xattn_a1_wq': 8.0,
     'L1_xattn_a1_wk': 8.0,
     'L1_xattn_a1_wv': 6.362,
     'L1_xattn_a1_li1_w': 6.378,
     'L1_xattn_a1_li2_w': 3.466,
     'L1_xattn_a1_li3_w': 3.189,
     'L1_xattn_a2_wq': 8.0,
     'L1_xattn_a2_wk': 8.0,
     'L1_xattn_a2_wv': 4.441,
     'L1_xattn_a2_li1_w': 4.448,
     'L1_xattn_a2_li2_w': 3.252,
     'L1_xattn_a2_li3_w': 2.965,
     'L1_ffn_router_w': 8.0,
     'L1_ffn_w1': 8.0,
     'L1_ffn_w2': 8.0}
    for name, (base, spread) in spreads.items():
        noise = np.random.default_rng([zlib.crc32(name.encode()), seed]).standard_normal(out[name].shape)
        drawn = base * np.exp(spread * noise) if base else spread * noise
        out[name] = jnp.asarray(drawn.astype(out[name].dtype))
    for name, factor in factors.items():
        out[name] = (out[name] * factor).astype(out[name].dtype)
    return out
```

```python
import concourse.bass as bass
from concourse import mybir
from contextlib import ExitStack

F32 = mybir.dt.float32
BF16 = mybir.dt.bfloat16
I32 = mybir.dt.int32
U32 = mybir.dt.uint32
ALU = mybir.AluOpType
ACT = mybir.ActivationFunctionType
AX = mybir.AxisListType

P = 128
TOK = 128
CTX = 120
LAT = 64
HEADS = 16
NG = 4
D0 = 8
D1 = 32
E0, FF0 = 8, 512
E1, TOPK, CAP, I1 = 64, 4, 128, 64
EPS = 1e-5


def positive(n):
    return not isinstance(n, int) or n > 0


class Unit:

    def __init__(self, base, i, per, r):
        self.base, self.i, self.per, self.r = base, i, per, r

    def count(self, each, k=0):
        return self.i * (self.per * each) + ((self.base + self.r) * each + k)

    def shift(self, d):
        return Unit(self.base, self.i, self.per, self.r + d)


def build_program(nc, t, out, NB=64):
    NTOK = NB * TOK
    TILES0 = NB + E0
    PAD0 = NTOK
    SLOTS0 = E0 * NTOK + TILES0 * P
    SLOTS1 = E1 * CAP
    CROWS = TOPK * NTOK

    xn0_d = nc.dram_tensor("xn0_d", (NTOK + P, P), F32).ap()
    y0_d = nc.dram_tensor("y0_d", (NTOK, P), F32).ap()
    list0_d = nc.dram_tensor("list0_d", (SLOTS0, 1), I32).ap()
    xn1_d = nc.dram_tensor("xn1_d", (NTOK, P), F32).ap()
    list1_d = nc.dram_tensor("list1_d", (SLOTS1, 2), F32).ap()
    c_d = nc.dram_tensor("c_d", (CROWS, P), F32).ap()
    y127_d = nc.dram_tensor("y127_d", (E1, P), F32).ap()

    ctx = ExitStack()
    with ctx:
        def sb(name, shape, dt=F32):
            return ctx.enter_context(nc.sbuf_tensor(name, shape, dt))

        def sem(name):
            return ctx.enter_context(nc.semaphore(name))

        xres = sb("xres", [P, NB, P])
        ctx_sb = sb("ctx_sb", [CTX, NB, LAT])
        pover = sb("pover", [P, NB, E1])
        big = sb("big", [P, 12288])
        w1T0 = big[:, 0:4096].rearrange("p (e f) -> p e f", e=E0)
        w2T0 = big[:, 4096:8192].rearrange("p (e c d) -> p e c d", e=E0, c=4)
        b1bc0 = big[:, 8192:12288].rearrange("p (e f) -> p e f", e=E0)
        w1_1 = big[:, 0:8192].rearrange("p (e f) -> p e f", e=E1)
        w2_1 = big[:, 8192:12288].rearrange("p (e h) -> p e h", e=E1 // 2)
        b2bc0 = sb("b2bc0", [P, E0, P])

        cst = sb("cst", [P, CST_WIDTH])
        cst_i = sb("cst_i", [P, CSTI_WIDTH], I32)
        ident = cst[:, 0:128]
        ltri_f = cst[:, 128:256]
        ones_h = cst[:, 256:384].rearrange("p (g c) -> p g c", g=NG)
        ones32 = cst[:, 384:416]
        iota64 = cst[:, 416:480]
        slot0 = cst[:, 480:488]
        kmask = cst[:, 488:492]
        neghalf = cst[:, 493:494]
        tilenum = cst[0:1, 494:494 + TILES0]
        padlist0 = cst_i[:, 0:128]
        padlist1 = cst_i[:, 128:256]
        tokid = cst_i[:, 256:258]
        ltri = sb("ltri", [P, P], BF16)
        onesb = sb("onesb", [P, P], BF16)
        zeros = sb("zeros", [P, P])

        wqT0 = sb("wqT0", [P, P])
        wkvT0 = sb("wkvT0", [LAT, 2 * P])
        woT0 = sb("woT0", [P, P])
        wrT0 = sb("wrT0", [P, E0])
        br0 = sb("br0", [P, E0])
        rw1 = sb("rw1", [P, E1])
        wq, wk, wv, li1, li2, li3, bv = ([sb(f"{n}{a}", [P, 512]) for a in (1, 2)]
                                         for n in ("wq", "wk", "wv", "li1", "li2", "li3", "bv"))
        bq, bk, b2c = ([sb(f"{n}{a}", [P, 4]) for a in (1, 2)] for n in ("bq", "bk", "b2c"))
        li1b, li3b, g_ln, b_ln = ([sb(f"{n}{a}", [P, P]) for a in (1, 2)]
                                  for n in ("li1b", "li3b", "g_ln", "b_ln"))
        cols = sb("cols", [P, 2, 6])

        qT = sb("qT", [P, 2, 512])
        kT = sb("kT", [P, 2, 512])
        vS = sb("vS", [P, 2, 512])
        nmax = sb("nmax", [P, 2, 4])
        prob = sb("prob", [P, 2, 512])
        pT = sb("pT", [P, 2, 512])
        pTm = sb("pTm", [P, 2, 512])
        rden = sb("rden", [P, 512])
        oT = sb("oT", [P, 2, 512])

        zS = sb("zS", [P, P])
        zT = sb("zT", [P, P])
        cS = sb("cS", [CTX, LAT])
        cT = sb("cT", [LAT, CTX])
        yb = sb("yb", [P, 2, P])
        tmp = sb("tmp", [P, P])
        xx = sb("xx", [P, 2, P])
        xxb = sb("xxb", [P, 2, P])
        xo = sb("xo", [P, P])
        ss = sb("ss", [P, P])
        ssa = sb("ssa", [P, P])
        xp = sb("xp", [P, P])
        z3 = sb("z3", [P, P])
        z3T = sb("z3T", [P, P])
        hT = sb("hT", [P, 512])
        xnS = sb("xnS", [P, 2, P])
        xnT = sb("xnT", [P, P])
        st_h, st_x, st_c, st_3, st_n = (sb(n, [P, 10]) for n in
                                        ("st_h", "st_x", "st_c", "st_3", "st_n"))
        lg = sb("lg", [P, E1])
        v8 = sb("v8", [P, 8])
        i8 = sb("i8", [P, 8], U32)
        i8f = sb("i8f", [P, 4])
        nv0 = sb("nv0", [P, 1])
        expl = sb("expl", [P, E1])
        esum = sb("esum", [P, 1])
        rsum = sb("rsum", [P, 1])
        e4 = sb("e4", [P, 4])
        oh4 = sb("oh4", [P, TOPK, E1])
        oh4s = sb("oh4s", [P, TOPK, E1])
        mask_b = sb("mask_b", [P, E1], BF16)
        mask_f = sb("mask_f", [P, E1])
        count0 = sb("count0", [P, E0])
        count1 = sb("count1", [P, E1])
        pos = sb("pos", [P, E1])
        posw = sb("posw", [P, E1])
        over = sb("over", [P, E1])
        dest_f = sb("dest_f", [P, 4])
        dest = sb("dest", [P, 2, 4], U32)
        pay = sb("pay", [P, 2, TOPK, 2])
        pay_i = pay[:, :, :, :].bitcast(I32)

        RING = 4
        ids = sb("ids", [P, RING], I32)
        idr = sb("idr", [P, RING], I32)
        wcol = sb("wcol", [P, RING])
        xg = qT[:, :, :].rearrange("p a (b d) -> p (a b) d", d=P)[:, 0:RING, :]
        yS = qT[:, :, :].rearrange("p a (b d) -> p (a b) d", d=P)[:, RING:2 * RING, :]
        xgT = pTm[:, 0, :].rearrange("p (b d) -> p b d", d=P)[:, 0:2, :]
        silu = pTm[:, 1, :].rearrange("p (b d) -> p b d", d=P)[:, 0:2, :]
        glu = pTm[:, 1, :].rearrange("p (b d) -> p b d", d=P)[:, 2:4, :]
        h0, h0T = prob, pT
        ylast = kT[:, :, :].rearrange("p a (b d) -> p (a b) d", d=P)[:, 0:RING, :]
        mp = oT[0:1, :, :].rearrange("p a b -> p (a b)")[:, 0:TILES0 * 7].rearrange("p (j e) -> p j e", e=7)
        mp2 = vS[0:1, :, :].rearrange("p a b -> p (a b)")[:, 0:TILES0 * 7].rearrange("p (j e) -> p j e", e=7)
        nt_i = sb("nt_i", [1, E0], I32)
        nt_f = sb("nt_f", [1, E0])
        ends = sb("ends", [1, E0])
        etile = sb("etile", [1, TILES0])
        stile = sb("stile", [1, TILES0])
        btile = sb("btile", [1, TILES0])
        etile_i = sb("etile_i", [1, TILES0], I32)
        base_i = sb("base_i", [1, TILES0], I32)
        list1 = sb("list1", [P, E1 + 2, 2])
        list1_i = list1[:, :, :].bitcast(I32)
        y127 = sb("y127", [E1, P])
        cb = [vS[:, 0, :], vS[:, 1, :], oT[:, 0, :], oT[:, 1, :]]
        poS = pT[:, 0, :].rearrange("p (b d) -> p b d", d=P)
        poT = pT[:, 1, :].rearrange("p (b d) -> p b d", d=P)
        csum2 = prob
        acc = pTm[:, 0, :].rearrange("p (b d) -> p b d", d=P)
        acc2 = pTm[:, 1, :].rearrange("p (b d) -> p b d", d=P)
        outS = kT[:, 0, :].rearrange("p (b d) -> p b d", d=P)

        bank = [ctx.enter_context(nc.psum_tensor(f"bank{i}", [P, 512], F32)) for i in range(8)]
        sbank, tbank = bank[0:2], bank[2:4]
        obank, dbank = bank[4], bank[5]
        m0, m1 = bank[6], bank[7]

        s_const = sem("s_const")
        s_load = sem("s_load")
        s_x = [sem("s_x_first"), sem("s_x_rest")]
        s_ffnw = sem("s_ffnw")
        s_made = sem("s_made")
        s_init = sem("s_init")
        s_c0 = sem("s_c0")
        s_prep = sem("s_prep")
        s_prep_pe = sem("s_prep_pe")
        s_q, s_k, s_v = sem("s_q"), sem("s_k"), sem("s_v")
        s_s = sem("s_s")
        s_max = sem("s_max")
        s_exp = sem("s_exp")
        s_tr = sem("s_tr")
        s_pt = [sem("s_pt_even"), sem("s_pt_odd")]
        s_ptm = sem("s_ptm")
        s_pv = sem("s_pv")
        s_oT = sem("s_oT")
        s_hvar, s_hrstd = sem("s_hvar"), sem("s_hrstd")
        s_xvar, s_xrstd = sem("s_xvar"), sem("s_xrstd")
        s_cvar, s_crstd = sem("s_cvar"), sem("s_crstd")
        s_z, s_c = sem("s_z"), sem("s_c")
        s_ht = sem("s_ht")
        s_zT = sem("s_zT")
        s_qps, s_kps, s_vps = sem("s_qps"), sem("s_kps"), sem("s_vps")
        s_xx, s_xxb = sem("s_xx"), sem("s_xxb")
        s_y0 = [sem("s_y0_even"), sem("s_y0_odd")]
        s_x2 = sem("s_x2")
        s_li1 = sem("s_li1")
        s_xo = sem("s_xo")
        s_3var, s_3rstd = sem("s_3var"), sem("s_3rstd")
        s_z3, s_z3t, s_z3T = sem("s_z3"), sem("s_z3t"), sem("s_z3T")
        s_li2, s_gelu, s_li3 = sem("s_li2"), sem("s_gelu"), sem("s_li3")
        s_ss = sem("s_ss")
        s_nvar, s_nrstd = sem("s_nvar"), sem("s_nrstd")
        s_xn, s_xnt, s_xnT = sem("s_xn"), sem("s_xnt"), sem("s_xnT")
        s_lgps = sem("s_lgps")
        s_v8 = sem("s_v8")
        s_el = sem("s_el")
        s_mask = sem("s_mask")
        s_cum = sem("s_cum")
        s_cumr = sem("s_cumr")
        s_dest = sem("s_dest")
        s_xnd = [sem("s_xnd_even"), sem("s_xnd_odd")]
        s_sc = [sem("s_sc_even"), sem("s_sc_odd")]
        s_sc1 = [sem("s_sc1_even"), sem("s_sc1_odd")]
        s_map = sem("s_map")
        s_ids = [sem(f"s_ids{k}") for k in range(RING)]
        s_idx = sem("s_idx")
        s_g = [sem(f"s_g{k}") for k in range(RING)]
        s_gt, s_gT = sem("s_gt"), sem("s_gT")
        s_hps, s_h = sem("s_hps"), sem("s_h")
        s_htr, s_hT = sem("s_htr"), sem("s_hT")
        s_yps, s_y = sem("s_yps"), sem("s_y")
        s_ysc = [sem(f"s_ysc{k}") for k in range(RING)]
        s_w1 = sem("s_w1")
        s_l1 = sem("s_l1")
        s_sil = sem("s_sil")
        s_yl = sem("s_yl")
        s_y127d = sem("s_y127d")
        s_yld = [sem(f"s_yld{k}") for k in range(RING)]
        s_cld = [sem(f"s_cld{k}") for k in range(RING)]
        s_po, s_pot, s_poT = sem("s_po"), sem("s_pot"), sem("s_poT")
        s_ov, s_acc, s_cs, s_fin = sem("s_ov"), sem("s_acc"), sem("s_cs"), sem("s_fin")
        s_out = [sem(f"s_out{k}") for k in range(RING)]

        RA, RB = NB // 2, NB // 2
        N_LOADS = 5 + 1 + 2 * 17
        FIRST = 4
        NINIT = -(-(SLOTS0 // P) // P) + 2

        def rounds(eng, n_rounds, base, per, prologue, half, epilogue, before_loop=None):
            prologue(Unit(base, 0, per, 0))
            for r in range(per):
                half(Unit(base, 0, per, r), r, r > 0, True)
            if before_loop:
                before_loop()
            with eng.Fori(1, n_rounds - 1) as i:
                for r in range(per):
                    half(Unit(base, i, per, r), r, True, True)
            last = n_rounds - 1
            for r in range(per):
                half(Unit(base, last, per, r), r, True, r < per - 1)
            epilogue(Unit(base, last, per, per - 1))

        def batch_unit(base, u):
            return Unit(base, u.i, 2, 2 * (u.r // 4) + u.r % 2)

        def ring_rounds(eng, n, step, after):
            for k in range(RING):
                step(0, k, True)
            with eng.Fori(1, n // RING) as i:
                for k in range(RING):
                    step(i, k, False)
            after(n // RING - 1)

        block = ctx.enter_context(nc.Block())

        @block.sync
        def _(sp):
            x_v = t["x"].rearrange("b s d -> s b d")
            c_v = t["ctx"].rearrange("b s d -> s b d")
            sp.dma_start(cst[:, :], t["cst"]).then_inc(s_const, 16)
            sp.dma_start(cst_i[:, :], t["cst_i"]).then_inc(s_const, 16)
            sp.dma_start(xres[:, 0:FIRST, :], x_v[:, 0:FIRST, :]).then_inc(s_x[0], 16)
            sp.dma_start(ctx_sb[:, 0:FIRST, :], c_v[:, 0:FIRST, :]).then_inc(s_x[0], 16)
            for dst, name in ((wqT0, "wqT0"), (wkvT0, "wkvT0"), (woT0, "woT0"), (wrT0, "wrT0"),
                              (rw1, "router")):
                sp.dma_start(dst[:, :], t[name]).then_inc(s_load, 16)
            sp.dma_start(br0[:, :], t["br0"].partition_broadcast(P)).then_inc(s_load, 16)
            sp.dma_start(xres[:, FIRST:NB, :], x_v[:, FIRST:NB, :]).then_inc(s_x[1], 16)
            sp.dma_start(ctx_sb[:, FIRST:NB, :], c_v[:, FIRST:NB, :]).then_inc(s_x[1], 16)
            for a in range(2):
                for n, dst in (("wq", wq), ("wk", wk), ("wv", wv), ("li1", li1), ("li2", li2),
                               ("li3", li3), ("b2c", b2c)):
                    rows = LAT if (a == 1 and n in ("wk", "wv")) else P
                    sp.dma_start(dst[a][0:rows, :], t[f"{n}{a}"]).then_inc(s_load, 16)
                for n, dst in (("li1b", li1b), ("li3b", li3b), ("g_ln", g_ln), ("b_ln", b_ln)):
                    sp.dma_start(dst[a][:, :], t[f"{n}{a}"].partition_broadcast(P)).then_inc(s_load, 16)
                for k, n in enumerate(("lnxg", "lnxb", "lnyg", "lnyb", "ln3g", "ln3b")):
                    rows = LAT if (a == 1 and n.startswith("lny")) else P
                    sp.dma_start(cols[0:rows, a, k:k + 1], t[f"{n}{a}"]).then_inc(s_load, 16)
            sp.wait_ge(s_const, 32)
            sp.wait_ge(s_made, 1)
            rows = SLOTS0 // P
            list0_rows = list0_d.rearrange("(r q) o -> r (q o)", q=P)
            for at in range(0, rows, P):
                n = min(P, rows - at)
                sp.dma_start(list0_rows[at:at + n, :], padlist0[0:n, :]).then_inc(s_init, 16)
            list1_v = list1_d.rearrange("(p e) c -> p (e c)", e=E1)
            sp.dma_start(list1_v, padlist1[:, :].bitcast(F32)).then_inc(s_init, 16)
            sp.dma_start(xn0_d[NTOK:NTOK + P, :], zeros[:, :]).then_inc(s_init, 16)
            sp.dma_start(w1T0, t["w1T0"]).then_inc(s_ffnw, 16)
            sp.dma_start(w2T0, t["w2T0"]).then_inc(s_ffnw, 16)
            sp.dma_start(b1bc0, t["b10"].partition_broadcast(P)).then_inc(s_ffnw, 16)
            sp.dma_start(b2bc0[:, :, :], t["b20"].partition_broadcast(P)).then_inc(s_ffnw, 16)

            c_rows = c_d.rearrange("(n p a) d -> n p a d", p=P, a=4)
            zeros4 = zeros[:, :].unsqueeze(1).to_broadcast([P, 4, P])
            n_c = CROWS // (4 * P)

            def store_xn(v, dst):
                sp.wait_ge(s_xn, v.count(1, 1))
                sp.nop(nofuse=True)
                s = v.r % 2
                b = v.i * 2 + v.r
                sp.dma_start(dst[bass.ds(b * P, P), :], xnS[:, s, :]).then_inc(s_xnd[s], 16)

            def half_a(u, r, tail, head):
                if r == 0:
                    for k in range(n_c // RA):
                        sp.dma_start(c_rows[u.i * (n_c // RA) + k], zeros4).then_inc(s_c0, 16)
                if tail:
                    store_xn(u.shift(-1), xn0_d)

            rounds(sp, RA, 0, 2, lambda u: None, half_a, lambda u: store_xn(u, xn0_d))

            for s in range(2):
                sp.wait_ge(s_sc[s], 16 * (NB // 2))
            sp.wait_ge(s_map, 1)

            def tile_ids(i, k, first):
                at = sp.value_load(base_i[0:1, bass.ds(i * RING + k, 1)], min_val=0,
                                   max_val=SLOTS0 - P)
                if positive(n := i * 16):
                    sp.wait_ge(s_ysc[k], n)
                    sp.nop(nofuse=True)
                sp.dma_start(ids[:, k:k + 1], list0_d[bass.ds(at, P), :]).then_inc(s_ids[k], 16)

            ring_rounds(sp, TILES0, tile_ids, lambda last: None)

            for k in range(RING):
                sp.wait_ge(s_ysc[k], 16 * (TILES0 // RING))
            sp.wait_ge(s_y, TILES0)
            sp.dma_start(w1_1, t["w1_1"]).then_inc(s_w1, 16)
            sp.dma_start(w2_1, t["w2_1"]).then_inc(s_w1, 16)

            def load_y0(h):
                hb = batch_unit(0, h)
                s = hb.r % 2
                b = hb.i * 2 + hb.r
                if positive(n := hb.count(1, -1)):
                    sp.wait_ge(s_x2, n)
                    sp.nop(nofuse=True)
                sp.dma_start(yb[:, s, :], y0_d[bass.ds(b * P, P), :]).then_inc(s_y0[s], 16)

            def half_b(u, r, tail, head):
                if head and r in (0, 3):
                    load_y0(u.shift(1))
                if tail and r in (0, 3):
                    v = batch_unit(NB, u.shift(-1))
                    store_xn(v, xn1_d)

            rounds(sp, RB, NB, 4, load_y0, half_b,
                   lambda u: store_xn(batch_unit(NB, u), xn1_d))

            for s in range(2):
                sp.wait_ge(s_sc1[s], 64 * (NB // 2))
            sp.dma_start(list1[:, 0:E1, :], list1_d.rearrange("(p e) c -> p e c", e=E1))\
                .then_inc(s_l1, 16)

            def store_last(i, k, first):
                sp.wait_ge(s_yl, i * RING + k + 1)
                sp.nop(nofuse=True)
                sp.dma_start(y127_d[bass.ds(i * RING + k, 1), :], ylast[127:128, k, :])\
                    .then_inc(s_yld[k], 16)

            ring_rounds(sp, E1, store_last, lambda last: None)
            for k in range(RING):
                sp.wait_ge(s_yld[k], 16 * (E1 // RING))
            sp.dma_start(y127[:, :], y127_d).then_inc(s_y127d, 16)

            for k in range(RING):
                sp.wait_ge(s_ysc[k], 16 * ((TILES0 + E1) // RING))
            c_v4 = c_d.rearrange("(k t) d -> t k d", k=TOPK)

            def load_c(i, k):
                if positive(n := (i * RING + k) - RING + 1):
                    sp.wait_ge(s_cs, n)
                    sp.nop(nofuse=True)
                sp.dma_start(cb[k].rearrange("p (k d) -> p k d", k=TOPK),
                             c_v4[bass.ds((i * RING + k) * P, P), :, :]).then_inc(s_cld[k], 16)

            def store_out(i, k):
                sp.wait_ge(s_fin, i * RING + k + 1)
                sp.nop(nofuse=True)
                sp.dma_start(out[bass.ds((i * RING + k) * P, P), :], outS[:, k, :])\
                    .then_inc(s_out[k], 16)

            for k in range(RING):
                load_c(0, k)
            with sp.Fori(0, NB // RING - 1) as i:
                for k in range(RING):
                    store_out(i, k)
                    load_c(i + 1, k)
            for k in range(RING):
                store_out(NB // RING - 1, k)
            for k in range(RING):
                sp.wait_ge(s_out[k], 16 * (NB // RING))
            sp.wait_ge(s_c0, 16 * n_c)
            for s in range(2):
                sp.wait_ge(s_xnd[s], 16 * NB)

        @block.tensor
        def _(pe):
            mm, tr = nc.tensor.matmul, nc.tensor.transpose

            def scores(u, g, width):
                s = u.r % 2
                if g == 0:
                    pe.wait_ge(s_q, u.count(1, 1))
                    pe.wait_ge(s_k, u.count(1, 1))
                if positive(n := u.count(4, g - 1)):
                    pe.wait_ge(s_exp, n)
                rows = slice(32 * g, 32 * g + 32)
                o = sbank[g % 2]
                if width == 0:
                    last = mm(o[:, 0:4 * CTX], qT[rows, s, 0:P], kT[rows, s, 0:4 * CTX],
                              start=True, stop=True)
                else:
                    for c in range(4):
                        last = mm(o[:, c * width:(c + 1) * width], qT[rows, s, c * P:(c + 1) * P],
                                  kT[rows, s, c * width:(c + 1) * width], start=True, stop=True)
                last.then_inc(s_s, 1)

            def transposes(u, g, T):
                pe.wait_ge(s_exp, u.count(4, g + 1))
                if positive(n := u.count(2, g // 2)):
                    pe.wait_ge(s_pt[g % 2], n)
                for c in range(4):
                    last = tr(tbank[g % 2][0:T, c * P:(c + 1) * P],
                              prob[:, g % 2, c * T:(c + 1) * T], ident)
                last.then_inc(s_tr, 1)

            def values0(u, g):
                s = u.r % 2
                pe.wait_ge(s_pt[g % 2], u.count(2, g // 2 + 1))
                if g == 0:
                    pe.wait_ge(s_v, u.count(1, 1))
                    if positive(n := u.count(1, 0)):
                        pe.wait_ge(s_oT, n)
                for o in (obank, dbank):
                    for j in range(4):
                        lhsT = (vS[0:CTX, s, (4 * g + j) * 32:(4 * g + j + 1) * 32] if o is obank
                                else ones_h[0:CTX, g, :])
                        last = mm(o[32 * j:32 * j + 32, 0:P], lhsT, pT[0:CTX, g % 2, j * P:(j + 1) * P],
                                  start=(g == 0), stop=(g == 3))
                last.then_inc(s_pv, 1)

            def values1(u, g, T, masked):
                s = u.r % 2
                pe.wait_ge(s_pt[g % 2], u.count(2, g // 2 + 1))
                if g == 0:
                    pe.wait_ge(s_v, u.count(1, 1))
                    pe.wait_ge(s_oT, u.count(1, 0))
                if masked:
                    pe.wait_ge(s_ptm, batch_unit(0, u).count(4, g + 1))
                w = pTm if masked else pT
                for c in range(4):
                    mm(obank[32 * c:32 * c + 32, g * P:(g + 1) * P],
                       vS[0:T, s, (4 * c + g) * 32:(4 * c + g + 1) * 32],
                       w[0:T, g % 2, c * P:(c + 1) * P], start=True, stop=True)
                for c in range(4):
                    last = mm(dbank[32 * c:32 * c + 32, g * P:(g + 1) * P], ones32[0:T, :],
                              pT[0:T, g % 2, c * P:(c + 1) * P], start=True, stop=True)
                last.then_inc(s_pv, 1)

            def router_transpose(v, b):
                pe.wait_ge(s_xn, v.count(1, 1))
                tr(b[:, 0:P], xnS[:, v.r % 2, :], ident).then_inc(s_xnt, 1)

            def router_logits(v, b, w, n):
                pe.wait_ge(s_xnT, v.count(1, 1))
                mm(b[:, 0:n], xnT[:, :], w[:, :], start=True, stop=True).then_inc(s_lgps, 1)

            def router_counts(v, b, n):
                pe.wait_ge(s_mask, v.count(1, 1))
                mm(b[:, 0:n], ltri[:, :], mask_b[:, 0:n], start=True, stop=True)
                mm(b[:, n:2 * n], onesb[:, :], mask_b[:, 0:n], start=True, stop=True)\
                    .then_inc(s_cum, 1)

            pe.wait_ge(s_const, 32)
            pe.wait_ge(s_load, 16 * N_LOADS)
            pe.wait_ge(s_made, 3)

            def head_a(h):
                s = h.r % 2
                pe.wait_ge(s_z, h.count(1, 1))
                pe.wait_ge(s_c, h.count(1, 1))
                tr(m0[:, 0:P], zS[:, :], ident)
                tr(m0[0:LAT, P:P + CTX], cS[:, :], ident[0:CTX, 0:CTX]).then_inc(s_ht, 1)
                pe.wait_ge(s_zT, h.count(1, 1))
                if positive(n := h.count(1, -1)):
                    pe.wait_ge(s_cumr, n)
                mm(m1[:, 0:P], wqT0[:, :], zT[:, :], start=True, stop=True)
                mm(m1[:, P:P + CTX], wkvT0[:, 0:P], cT[:, :], start=True, stop=True)
                mm(m1[0:CTX, 256:384], cT[:, :], wkvT0[:, P:2 * P], start=True, stop=True)\
                    .then_inc(s_qps, 1)

            def wo_a(v):
                pe.wait_ge(s_oT, v.count(1, 1))
                mm(m0[:, 0:P], oT[:, v.r % 2, 0:P], woT0[:, :], start=True, stop=True)\
                    .then_inc(s_li1, 1)

            def half_a(u, r, tail, head):
                v = u.shift(-1)
                scores(u, 0, 0)
                scores(u, 1, 0)
                if tail:
                    wo_a(v)
                transposes(u, 0, CTX)
                scores(u, 2, 0)
                values0(u, 0)
                if tail:
                    pe.wait_ge(s_v, u.count(1, 1))
                    router_transpose(v, m1)
                transposes(u, 1, CTX)
                scores(u, 3, 0)
                values0(u, 1)
                if tail:
                    router_logits(v, m0, wrT0, E0)
                transposes(u, 2, CTX)
                values0(u, 2)
                if tail:
                    router_counts(v, m1, E0)
                transposes(u, 3, CTX)
                values0(u, 3)
                if head:
                    head_a(u.shift(1))

            def tail_a(v):
                wo_a(v)
                router_transpose(v, m1)
                router_logits(v, m0, wrT0, E0)
                router_counts(v, m1, E0)

            rounds(pe, RA, 0, 2, head_a, half_a, tail_a)

            for a in range(2):
                rk = LAT if a else P
                pe.wait_ge(s_prep, 3 * a + 1)
                for c in range(4):
                    w = slice(c * P, (c + 1) * P)
                    mm(m0[:, c:c + 1], wq[a][:, w], cols[:, a, 1:2], start=True, stop=True)
                    mm(m0[:, 4 + c:5 + c], wk[a][0:rk, w], cols[0:rk, a, 3:4], start=True, stop=True)
                    mm(m0[:, 8 + c:9 + c], li2[a][:, w], cols[:, a, 5:6], start=True, stop=True)
                mm(m1[:, :], tmp[0:rk, :], wv[a][0:rk, :], start=True, stop=True).then_inc(s_prep_pe, 1)

            pe.wait_ge(s_map, 1)
            pe.wait_ge(s_ffnw, 64)

            def tokens_in(u, k, q):
                pe.wait_ge(s_g[k], u.count(4, 16 - 4 * k))
                if positive(n := u.count(1, -1)):
                    pe.wait_ge(s_gT, n)
                tr(bank[q][:, 0:P], xg[:, k, :], ident).then_inc(s_gt, 1)

            def expert(eng, i, k):
                return eng.value_load(etile_i[0:1, bass.ds(i * RING + k, 1)], min_val=0,
                                      max_val=E0 - 1)

            def hidden_t0(u, q):
                pe.wait_ge(s_h, u.count(1, 1))
                if positive(n := u.count(1, -1)):
                    pe.wait_ge(s_hT, n)
                for c in range(4):
                    last = tr(bank[4 + q][:, c * P:(c + 1) * P], h0[:, q, c * P:(c + 1) * P], ident)
                last.then_inc(s_htr, 1)

            def out0(u, q, e):
                pe.wait_ge(s_hT, u.count(1, 1))
                if positive(n := u.count(1, -1)):
                    pe.wait_ge(s_y, n)
                for c in range(4):
                    last = mm(bank[6 + q][:, 0:P], h0T[:, q, c * P:(c + 1) * P],
                              w2T0[:, bass.ds(e, 1), c, :].rearrange("p o d -> p (o d)"),
                              start=(c == 0), stop=(c == 3))
                last.then_inc(s_yps, 1)

            def tile0(i, k, first):
                u = Unit(0, i, RING, k)
                p = u.shift(-1)
                q = k % 2
                tokens_in(u, k, q)
                if not first or k > 0:
                    hidden_t0(p, 1 - q)
                e = expert(pe, i, k)
                pe.wait_ge(s_gT, u.count(1, 1))
                if positive(n := u.count(1, -1)):
                    pe.wait_ge(s_h, n)
                mm(bank[2 + q][:, :], xgT[:, q, :],
                   w1T0[:, bass.ds(e, 1), :].rearrange("p o f -> p (o f)"),
                   start=True, stop=True).then_inc(s_hps, 1)
                if not first or k > 0:
                    out0(p, 1 - q, expert(pe, i, k - 1))

            def end0(last):
                u = Unit(0, last, RING, RING - 1)
                hidden_t0(u, 1)
                out0(u, 1, expert(pe, last, RING - 1))

            ring_rounds(pe, TILES0, tile0, end0)

            pe.wait_ge(s_prep, 6)

            def head_b(h):
                l = Unit(0, h.i, 4, h.r)
                a = (h.r % 4) // 2
                hb = batch_unit(NB, h)
                rk, T = (LAT, CTX) if a else (P, TOK)
                pe.wait_ge(s_z, h.count(1, 1))
                if a == 0:
                    pe.wait_ge(s_cumr, hb.count(1, -1))
                    last = tr(m0[:, 0:P], zS[:, :], ident)
                else:
                    pe.wait_ge(s_c, hb.count(1, 1))
                    tr(m0[:, 0:P], zS[:, :], ident)
                    last = tr(m0[0:LAT, P:P + CTX], cS[:, :], ident[0:CTX, 0:CTX])
                last.then_inc(s_ht, 1)
                pe.wait_ge(s_zT, h.count(1, 1))
                y = cT if a else zT
                for c in range(4):
                    last = mm(m1[:, c * P:(c + 1) * P], wq[a][:, c * P:(c + 1) * P], zT[:, :],
                              start=True, stop=True)
                last.then_inc(s_qps, 1)
                for c in range(4):
                    last = mm(m0[:, c * T:(c + 1) * T], wk[a][0:rk, c * P:(c + 1) * P], y[:, :],
                              start=True, stop=True)
                last.then_inc(s_kps, 1)
                pe.wait_ge(s_q, h.count(1, 1))
                mm(m1[0:T, :], y[:, :], wv[a][0:rk, :], start=True, stop=True).then_inc(s_vps, 1)

            def li1_b(v):
                pe.wait_ge(s_oT, v.count(1, 1))
                a = (v.r % 4) // 2
                for g in range(4):
                    last = mm(m0[:, 0:P], oT[:, v.r % 2, g * P:(g + 1) * P],
                              li1[a][:, g * P:(g + 1) * P], start=(g == 0), stop=(g == 3))
                last.then_inc(s_li1, 1)

            def z3_b(v):
                pe.wait_ge(s_z3, Unit(0, v.i, 4, v.r).count(1, 1))
                tr(m1[:, 0:P], z3[:, :], ident).then_inc(s_z3t, 1)

            def li2_b(v):
                pe.wait_ge(s_z3T, Unit(0, v.i, 4, v.r).count(1, 1))
                a = (v.r % 4) // 2
                for c in range(4):
                    last = mm(m0[:, c * P:(c + 1) * P], li2[a][:, c * P:(c + 1) * P], z3T[:, :],
                              start=True, stop=True)
                last.then_inc(s_li2, 1)

            def li3_b(v):
                pe.wait_ge(s_gelu, Unit(0, v.i, 4, v.r).count(1, 1))
                a = (v.r % 4) // 2
                for c in range(4):
                    last = mm(m1[:, 0:P], hT[:, c * P:(c + 1) * P], li3[a][:, c * P:(c + 1) * P],
                              start=(c == 0), stop=(c == 3))
                last.then_inc(s_li3, 1)

            def route_b(v):
                if (v.r % 4) // 2:
                    vb = batch_unit(NB, v)
                    router_transpose(vb, m0)
                    router_logits(vb, m1, rw1, E1)
                    router_counts(vb, m0, E1)

            def half_b(u, r, tail, head):
                a = (r % 4) // 2
                T = CTX if a else TOK
                masked = a == 0
                v = u.shift(-1)
                scores(u, 0, T)
                scores(u, 1, T)
                if tail:
                    li1_b(v)
                transposes(u, 0, T)
                scores(u, 2, T)
                values1(u, 0, T, masked)
                if tail:
                    z3_b(v)
                transposes(u, 1, T)
                scores(u, 3, T)
                values1(u, 1, T, masked)
                if tail:
                    li2_b(v)
                transposes(u, 2, T)
                values1(u, 2, T, masked)
                transposes(u, 3, T)
                values1(u, 3, T, masked)
                if tail:
                    li3_b(v)
                    route_b(v)
                if head:
                    head_b(u.shift(1))

            def tail_b(v):
                pe.wait_ge(s_cumr, batch_unit(NB, v).count(1, 0))
                li1_b(v)
                z3_b(v)
                li2_b(v)
                li3_b(v)
                route_b(v)

            rounds(pe, RB, NB, 4, head_b, half_b, tail_b)

            pe.wait_ge(s_w1, 32)

            def glu_t(u, q):
                pe.wait_ge(s_h, u.count(1, 1))
                pe.wait_ge(s_hT, u.count(1, -1))
                pe.nop(nofuse=True)
                tr(bank[4 + q][:, 0:P], glu[:, q, :], ident).then_inc(s_htr, 1)

            def out1(u, q, i, k):
                pe.wait_ge(s_hT, u.count(1, 1))
                pe.wait_ge(s_y, u.count(1, -1))
                if positive(n := Unit(0, u.i, RING, u.r).count(1, -1)):
                    pe.wait_ge(s_yl, n)
                mm(bank[6 + q][:, 0:P], h0T[:, q, 0:P],
                   w2_1[:, bass.ds(i * (RING // 2) + k // 2, 1), :].rearrange("p o h -> p (o h)"),
                   start=True, stop=True).then_inc(s_yps, 1)

            def tile1(i, k, first):
                u = Unit(TILES0, i, RING, k)
                p = u.shift(-1)
                q = k % 2
                tokens_in(u, k, q)
                if not first or k > 0:
                    glu_t(p, 1 - q)
                pe.wait_ge(s_gT, u.count(1, 1))
                pe.wait_ge(s_h, u.count(1, -1))
                mm(bank[2 + q][:, 0:P], xgT[:, q, :],
                   w1_1[:, bass.ds(i * RING + k, 1), :].rearrange("p o f -> p (o f)"),
                   start=True, stop=True).then_inc(s_hps, 1)
                if not first or k > 0:
                    out1(p, 1 - q, i, k - 1)

            def end1(last):
                u = Unit(TILES0, last, RING, RING - 1)
                glu_t(u, 1)
                out1(u, 1, last, RING - 1)

            ring_rounds(pe, E1, tile1, end1)

            pe.wait_ge(s_y127d, 16)

            def step_c(i, k):
                u = Unit(0, i, RING, k)
                q = k % 2
                pe.wait_ge(s_po, u.count(1, 1))
                if positive(n := u.count(1, -1)):
                    pe.wait_ge(s_poT, n)
                    pe.nop(nofuse=True)
                tr(bank[q][0:E1, 0:P], poS[:, k, 0:E1], ident).then_inc(s_pot, 1)
                pe.wait_ge(s_poT, u.count(1, 1))
                if positive(n := u.count(1, -1)):
                    pe.wait_ge(s_acc, n)
                mm(bank[2 + q][:, 0:P], poT[0:E1, k, :], y127[:, :], start=True, stop=True)\
                    .then_inc(s_ov, 1)

            for k in range(RING):
                step_c(0, k)
            with pe.Fori(1, NB // RING) as i:
                for k in range(RING):
                    step_c(i, k)

        @block.scalar
        def _(act):
            af = nc.scalar.activation

            def exps(u, g, T):
                act.wait_ge(s_max, u.count(4, g + 1))
                if positive(n := u.count(4, g - 1)):
                    act.wait_ge(s_tr, n)
                for c in range(4):
                    last = af(prob[:, g % 2, c * T:(c + 1) * T], sbank[g % 2][:, c * T:(c + 1) * T],
                              ACT.Exp, bias=nmax[:, g % 2, c:c + 1])
                last.then_inc(s_exp, 1)

            def pt_even(u, g, T):
                act.wait_ge(s_tr, u.count(4, g + 1))
                if positive(n := u.count(4, g - 1)):
                    act.wait_ge(s_pv, n)
                af(pT[0:T, 0, :], tbank[0][0:T, :], ACT.Copy).then_inc(s_pt[0], 1)

            def core(u, T, between=None):
                exps(u, 0, T)
                exps(u, 1, T)
                pt_even(u, 0, T)
                exps(u, 2, T)
                exps(u, 3, T)
                pt_even(u, 2, T)

            act.wait_ge(s_x[0], 32)

            def head_a(h):
                if positive(n := h.count(1, 0)):
                    act.wait_ge(s_ht, n)
                    act.nop(nofuse=True)
                af(cS[:, :], ctx_sb[:, h.i * 2 + h.r, :], ACT.Copy).then_inc(s_c, 1)

            def half_a(u, r, tail, head):
                if head:
                    head_a(u.shift(1))
                core(u, CTX)

            rounds(act, RA, 0, 2, head_a, half_a, lambda u: None,
                   before_loop=lambda: act.wait_ge(s_x[1], 32))

            def relu(u, q):
                act.wait_ge(s_htr, u.count(1, 1))
                if positive(n := u.count(1, -1)):
                    act.wait_ge(s_yps, n)
                af(h0T[:, q, :], bank[4 + q][:, :], ACT.Relu).then_inc(s_hT, 1)

            ring_rounds(act, TILES0, lambda i, k, first: relu(Unit(0, i, RING, k), k % 2),
                        lambda last: None)

            def gelu(v):
                l = Unit(0, v.i, 4, v.r)
                a = (v.r % 4) // 2
                act.wait_ge(s_li2, l.count(1, 1))
                if positive(n := l.count(1, 0)):
                    act.wait_ge(s_li3, n)
                for c in range(4):
                    last = af(hT[:, c * P:(c + 1) * P], m0[:, c * P:(c + 1) * P], ACT.Gelu,
                              bias=b2c[a][:, c:c + 1])
                last.then_inc(s_gelu, 1)

            def route(v):
                if (v.r % 4) // 2:
                    vb = batch_unit(0, v)
                    act.wait_ge(s_v8, vb.count(1, 1))
                    af(expl[:, :], lg[:, :], ACT.Exp, bias=nv0[:, :], accum_out=esum[:, :])
                    af(e4[:, :], v8[:, 0:TOPK], ACT.Exp, bias=nv0[:, :]).then_inc(s_el, 1)

            def half_b(u, r, tail, head):
                core(u, CTX if r >= 2 else TOK)
                if tail:
                    gelu(u.shift(-1))
                    route(u.shift(-1))

            def tail_b(v):
                gelu(v)
                route(v)

            rounds(act, RB, NB, 4, lambda u: None, half_b, tail_b)

            def silu_part(u, q):
                act.wait_ge(s_hps, u.count(1, 1))
                act.wait_ge(s_h, u.count(1, -1))
                af(silu[:, q, 0:I1], bank[2 + q][:, 0:I1], ACT.Silu).then_inc(s_sil, 1)

            def last_slot(u, k, q):
                act.wait_ge(s_y, u.count(1, 1))
                af(ylast[96:128, k, :], bank[6 + q][96:128, 0:P], ACT.Copy).then_inc(s_yl, 1)

            def tile1(i, k, first):
                u = Unit(TILES0, i, RING, k)
                silu_part(u, k % 2)
                if positive(n := i * 16):
                    act.wait_ge(s_yld[k], n)
                if not first or k > 0:
                    last_slot(u.shift(-1), (k - 1) % RING, (k - 1) % 2)

            ring_rounds(act, E1, tile1,
                        lambda last: last_slot(Unit(TILES0, last, RING, RING - 1), RING - 1, 1))

            def step_c(i, k):
                u = Unit(0, i, RING, k)
                if positive(n := u.count(1, -3)):
                    act.wait_ge(s_pot, n)
                    act.nop(nofuse=True)
                af(poS[:, k, 0:E1], pover[:, bass.ds(i * RING + k, 1), :].rearrange("p o e -> p (o e)"),
                   ACT.Copy).then_inc(s_po, 1)
                act.wait_ge(s_pot, u.count(1, 1))
                if positive(n := u.count(1, -3)):
                    act.wait_ge(s_ov, n)
                af(poT[0:E1, k, :], bank[k % 2][0:E1, 0:P], ACT.Copy).then_inc(s_poT, 1)

            for k in range(RING):
                step_c(0, k)
            with act.Fori(1, NB // RING) as i:
                for k in range(RING):
                    step_c(i, k)

        @block.gpsimd
        def _(pool):
            g_ = nc.gpsimd

            def rstd(st, var, done, u, rows=P):
                pool.wait_ge(var, u.count(1, 1))
                pool.nop(nofuse=True)
                g_.tensor_tensor(st[0:rows, 9:10], st[0:rows, 8:9], neghalf[0:rows, :], ALU.pow)\
                    .then_inc(done, 1)

            pool.wait_ge(s_const, 32)

            def scatter_a(v):
                s = v.r % 2
                pool.wait_ge(s_dest, v.count(1, 1))
                pool.nop(nofuse=True)
                g_.indirect_dma_start(out=list0_d, out_offset=bass.IndirectOffsetOnAxis(
                    ap=dest[:, s, 0:1], axis=0), in_=tokid[:, s:s + 1], in_offset=None)\
                    .then_inc(s_sc[s], 16)

            def half_a(u, r, tail, head):
                if head:
                    rstd(st_h, s_hvar, s_hrstd, u.shift(1))
                if tail:
                    rstd(st_n, s_nvar, s_nrstd, u.shift(-1))
                    scatter_a(u.shift(-1))

            def first_a(u):
                rstd(st_h, s_hvar, s_hrstd, u)
                pool.wait_ge(s_init, 16 * NINIT)

            def last_a(v):
                rstd(st_n, s_nvar, s_nrstd, v)
                scatter_a(v)

            rounds(pool, RA, 0, 2, first_a, half_a, last_a)

            def gather(u, k, src, ready):
                ready(u, k)
                if positive(n := u.count(1, -3)):
                    pool.wait_ge(s_gt, n)
                    pool.nop(nofuse=True)
                g_.indirect_dma_start(out=xg[:, k, :], out_offset=None, in_=src,
                                      in_offset=bass.IndirectOffsetOnAxis(
                                          ap=ids[:, k:k + 1].bitcast(U32), axis=0))\
                    .then_inc(s_g[k], 16)

            def scatter(u, k, dst, idx):
                pool.wait_ge(s_y, u.count(1, 1))
                pool.nop(nofuse=True)
                g_.indirect_dma_start(out=dst, out_offset=bass.IndirectOffsetOnAxis(
                    ap=idx[:, k:k + 1].bitcast(U32), axis=0), in_=yS[:, k, :], in_offset=None,
                    bounds_check=dst.shape[0] - 1, oob_is_err=False)\
                    .then_inc(s_ysc[k], 16)

            def experts(n, base, src, dst, idx, ready):
                LAG = 2

                def step(i, k, first):
                    u = Unit(base, i, RING, k)
                    gather(u, k, src, ready)
                    if not first or k >= LAG:
                        scatter(u.shift(-LAG), (k - LAG) % RING, dst, idx)

                def after(last):
                    for k in range(RING - LAG, RING):
                        scatter(Unit(base, last, RING, k), k, dst, idx)

                ring_rounds(pool, n, step, after)

            for s in range(2):
                pool.wait_ge(s_xnd[s], 16 * (NB // 2))
            experts(TILES0, 0, xn0_d, y0_d, ids,
                    lambda u, k: pool.wait_ge(s_ids[k], u.i * 16 + 16))

            def head_first(h):
                rstd(st_h, s_hvar, s_hrstd, h)

            def head_second(h):
                l = Unit(0, h.i, 4, h.r)
                a = (h.r % 4) // 2
                s = h.r % 2
                pool.wait_ge(s_xx, l.count(1, 1))
                pool.nop(nofuse=True)
                if positive(n := l.count(1, -1)):
                    pool.wait_ge(s_xo, n)
                    pool.nop(nofuse=True)
                g_.tensor_tensor(xxb[:, s, :], xx[:, s, :], li1b[a][:, :], ALU.add).then_inc(s_xxb, 1)
                rstd(st_x, s_xvar, s_xrstd, l)

            def head_ctx(h):
                if (h.r % 4) // 2:
                    rstd(st_c, s_cvar, s_crstd, batch_unit(0, h), CTX)

            def tail_sum(v):
                l = Unit(0, v.i, 4, v.r)
                a = (v.r % 4) // 2
                s = v.r % 2
                pool.wait_ge(s_xo, l.count(1, 1))
                pool.nop(nofuse=True)
                g_.tensor_tensor(ssa[:, :], xx[:, s, :], xo[:, :], ALU.add)
                pool.drain()
                if a == 0:
                    g_.tensor_tensor(ss[:, :], ssa[:, :], li3b[a][:, :], ALU.add).then_inc(s_ss, 1)
                else:
                    vb = batch_unit(0, v)
                    g_.tensor_tensor(ss[:, :], ssa[:, :], li3b[a][:, :], ALU.add)
                    pool.drain()
                    g_.tensor_tensor(ss[:, :], ss[:, :], xres[:, vb.i * 2 + vb.r, :], ALU.add)\
                        .then_inc(s_ss, 1)

            def tail_rstd(v):
                rstd(st_3, s_3var, s_3rstd, Unit(0, v.i, 4, v.r))

            def mask_chunk(u, g):
                b = batch_unit(0, u)
                pool.wait_ge(s_pt[g % 2], u.count(2, g // 2 + 1))
                pool.nop(nofuse=True)
                pool.wait_ge(s_pv, u.count(4, g - 1))
                pool.nop(nofuse=True)
                g_.affine_select(out=pTm[:, g % 2, :], in_=pT[:, g % 2, :], compare_op=ALU.is_gt,
                                 fill=0.0, base=0, pattern=[[0, 4], [-1, P]],
                                 channel_multiplier=1).then_inc(s_ptm, 1)

            def scatter_b(v):
                vb = batch_unit(NB, v)
                s = vb.r % 2
                pool.wait_ge(s_dest, vb.count(1, 1))
                pool.nop(nofuse=True)
                for k in range(TOPK):
                    g_.indirect_dma_start(out=list1_d, out_offset=bass.IndirectOffsetOnAxis(
                        ap=dest[:, s, k:k + 1], axis=0), in_=pay[:, s, k, :], in_offset=None,
                        bounds_check=SLOTS1 - 1, oob_is_err=False)\
                        .then_inc(s_sc1[s], 16)

            def half_b(u, r, tail, head):
                masked = r < 2
                v, h = u.shift(-1), u.shift(1)
                if head:
                    head_ctx(h)
                if masked:
                    mask_chunk(u, 0)
                if tail:
                    tail_rstd(v)
                if masked:
                    mask_chunk(u, 1)
                if tail:
                    tail_sum(v)
                if head and r in (0, 3):
                    head_first(h)
                    if masked:
                        mask_chunk(u, 2)
                    head_second(h)
                elif masked:
                    mask_chunk(u, 2)
                if masked:
                    mask_chunk(u, 3)
                if tail and r in (0, 3):
                    rstd(st_n, s_nvar, s_nrstd, batch_unit(NB, v))
                    scatter_b(v)
                if head and r in (1, 2):
                    head_first(h)
                    head_second(h)

            def first_b(h):
                head_first(h)
                head_second(h)

            def last_b(v):
                tail_rstd(v)
                tail_sum(v)
                rstd(st_n, s_nvar, s_nrstd, batch_unit(NB, v))
                scatter_b(v)

            rounds(pool, RB, NB, 4, first_b, half_b, last_b)

            for s in range(2):
                pool.wait_ge(s_xnd[s], 16 * NB)
            pool.wait_ge(s_c0, 16 * (CROWS // (4 * P)))
            def indices_there(u, k):
                pool.wait_ge(s_idx, Unit(0, u.i, RING, u.r).count(1, 1))
                pool.nop(nofuse=True)

            experts(E1, TILES0, xn1_d, c_d, idr, indices_there)

            def step_c(i, k):
                u = Unit(0, i, RING, k)
                pool.wait_ge(s_cld[k], u.i * 16 + 16)
                pool.nop(nofuse=True)
                if positive(n := u.count(1, -1)):
                    pool.wait_ge(s_fin, n)
                    pool.nop(nofuse=True)
                g_.tensor_tensor(csum2[:, k % 2, 0:256], cb[k][:, 0:256], cb[k][:, 256:512],
                                 ALU.add).then_inc(s_cs, 1)

            for k in range(RING):
                step_c(0, k)
            with pool.Fori(1, NB // RING) as i:
                for k in range(RING):
                    step_c(i, k)

        @block.vector
        def _(dve):
            v_ = nc.vector

            def after():
                dve.drain()

            def copy(o, i):
                return v_.tensor_copy(o, i)

            def norm_stats(st, src, done, rows=P, a=1.0, c=EPS):
                v_.bn_stats(st[0:rows, 0:6], src)
                after()
                v_.bn_aggr(st[0:rows, 6:8], st[0:rows, 0:6])
                after()
                v_.tensor_scalar(st[0:rows, 8:9], st[0:rows, 7:8], a, c, ALU.mult, ALU.add)\
                    .then_inc(done, 1)

            def normalise(dst, src, st, rows=P):
                return v_.tensor_scalar(dst, src, st[0:rows, 6:7], st[0:rows, 9:10],
                                        ALU.subtract, ALU.mult)

            def maxima(u, g, T):
                dve.wait_ge(s_s, u.count(4, g + 1))
                if positive(n := u.count(4, g - 1)):
                    dve.wait_ge(s_exp, n)
                v_.tensor_reduce(nmax[:, g % 2, :],
                                 sbank[g % 2][:, 0:4 * T].rearrange("p (j t) -> p j t", j=4),
                                 AX.X, ALU.max, negate=True).then_inc(s_max, 1)

            def pt_odd(u, g, T):
                dve.wait_ge(s_tr, u.count(4, g + 1))
                if positive(n := u.count(4, g - 1)):
                    dve.wait_ge(s_pv, n)
                copy(pT[0:T, 1, :], tbank[1][0:T, :]).then_inc(s_pt[1], 1)

            def finish_core(u, width):
                dve.wait_ge(s_pv, u.count(4, 4))
                v_.reciprocal(rden[:, 0:width], dbank[:, 0:width])
                after()
                v_.tensor_tensor(oT[:, u.r % 2, 0:width], obank[:, 0:width], rden[:, 0:width],
                                 ALU.mult).then_inc(s_oT, 1)

            def bcast(col, n):
                return col.unsqueeze(2).to_broadcast([P, 4, n])

            v_.memset(zeros[:, :], 0.0).then_inc(s_made, 1)
            v_.memset(onesb[:, :], 1.0)
            v_.memset(count0[:, :], 0.0)
            v_.memset(count1[:, :], 0.0)
            v_.memset(vS[:, :, :], 0.0)
            dve.wait_ge(s_const, 32)
            copy(ltri[:, :], ltri_f).then_inc(s_made, 1)
            for s in range(2):
                copy(pay_i[:, s, :, 0], cst_i[:, 258 + 4 * s:262 + 4 * s])
            dve.wait_ge(s_load, 16 * N_LOADS)
            v_.tensor_scalar(wqT0[:, :], wqT0[:, :], float(D0) ** -0.5, None, ALU.mult)\
                .then_inc(s_made, 1)
            dve.wait_ge(s_x[0], 32)

            def head_stats_a(h):
                norm_stats(st_h, xres[:, h.i * 2 + h.r, :], s_hvar)

            def head_z_a(h):
                dve.wait_ge(s_hrstd, h.count(1, 1))
                normalise(zS[:, :], xres[:, h.i * 2 + h.r, :], st_h).then_inc(s_z, 1)

            def head_t_a(h):
                dve.wait_ge(s_ht, h.count(1, 1))
                copy(zT[:, :], m0[:, 0:P])
                copy(cT[:, :], m0[0:LAT, P:P + CTX]).then_inc(s_zT, 1)

            def head_qkv_a(h):
                s = h.r % 2
                dve.wait_ge(s_qps, h.count(1, 1))
                copy(qT[:, s, 0:P], m1[:, 0:P]).then_inc(s_q, 1)
                v_.tensor_tensor(kT[:, s, 0:4 * CTX].rearrange("p (j t) -> p j t", j=4),
                                 m1[:, P:P + CTX].unsqueeze(1).to_broadcast([P, 4, CTX]),
                                 bcast(kmask, CTX), ALU.mult).then_inc(s_k, 1)
                for g in range(4):
                    last = copy(vS[0:CTX, s, g * P:(g + 1) * P]
                                .rearrange("p (j c) -> p j c", j=4)[:, :, 8 * g:8 * g + 8],
                                m1[0:CTX, 256 + 32 * g:288 + 32 * g].rearrange("p (j d) -> p j d", j=4))
                last.then_inc(s_v, 1)

            def tail_x_a(v):
                b = v.i * 2 + v.r
                dve.wait_ge(s_li1, v.count(1, 1))
                v_.tensor_tensor(xres[:, b, :], xres[:, b, :], m0[:, 0:P], ALU.add)
                after()
                norm_stats(st_n, xres[:, b, :], s_nvar)

            def tail_xn(v, b):
                s = v.r % 2
                dve.wait_ge(s_nrstd, v.count(1, 1))
                normalise(xnS[:, s, :], xres[:, b, :], st_n).then_inc(s_xn, 1)

            def tail_xnT(v, b):
                dve.wait_ge(s_xnt, v.count(1, 1))
                copy(xnT[:, :], b[:, 0:P]).then_inc(s_xnT, 1)

            def tail_choose_a(v):
                dve.wait_ge(s_lgps, v.count(1, 1))
                v_.tensor_tensor(lg[:, 0:E0], m0[:, 0:E0], br0[:, :], ALU.add)
                after()
                v_.max(out=v8[:, :], in_=lg[:, 0:E0])
                after()
                v_.max_index(i8[:, :], v8[:, :], lg[:, 0:E0])
                after()
                copy(i8f[:, 0:1], i8[:, 0:1])
                after()
                v_.tensor_scalar(mask_f[:, 0:E0], iota64[:, 0:E0], i8f[:, 0:1], None, ALU.is_equal)
                v_.tensor_scalar(mask_b[:, 0:E0], iota64[:, 0:E0], i8f[:, 0:1], None, ALU.is_equal)\
                    .then_inc(s_mask, 1)

            def tail_dest_a(v):
                s = v.r % 2
                dve.wait_ge(s_cum, v.count(1, 1))
                v_.tensor_tensor(pos[:, 0:E0], m1[:, 0:E0], count0[:, :], ALU.add)
                after()
                v_.tensor_tensor(count0[:, :], m1[:, E0:2 * E0], count0[:, :], ALU.add)\
                    .then_inc(s_cumr, 1)
                v_.tensor_tensor(posw[:, 0:E0], pos[:, 0:E0], slot0, ALU.add)
                after()
                v_.tensor_tensor(pos[:, 0:E0], posw[:, 0:E0], mask_f[:, 0:E0], ALU.mult)
                after()
                v_.tensor_reduce(dest_f[:, 0:1], pos[:, 0:E0], AX.X, ALU.add)
                after()
                v_.tensor_scalar(tokid[:, s:s + 1], tokid[:, s:s + 1], 2.0 * P, None, ALU.add)
                copy(dest[:, s, 0:1], dest_f[:, 0:1]).then_inc(s_dest, 1)

            def slots_free_a(u):
                if positive(n := u.i * 16):
                    dve.wait_ge(s_xnd[u.r % 2], n)
                if positive(n := u.i * 16):
                    dve.wait_ge(s_sc[u.r % 2], n)

            def half_a(u, r, tail, head):
                v, h = u.shift(-1), u.shift(1)
                if head:
                    head_stats_a(h)
                maxima(u, 0, CTX)
                maxima(u, 1, CTX)
                if tail:
                    tail_x_a(v)
                if head:
                    head_z_a(h)
                if tail:
                    tail_xn(v, v.i * 2 + v.r)
                maxima(u, 2, CTX)
                if tail:
                    tail_xnT(v, m1)
                pt_odd(u, 1, CTX)
                maxima(u, 3, CTX)
                if tail:
                    tail_choose_a(v)
                    tail_dest_a(v)
                pt_odd(u, 3, CTX)
                if head:
                    head_t_a(h)
                finish_core(u, P)
                slots_free_a(u)
                if head:
                    head_qkv_a(h)

            def first_a(h):
                head_stats_a(h)
                head_z_a(h)
                head_t_a(h)
                head_qkv_a(h)

            def last_a(v):
                tail_x_a(v)
                tail_xn(v, v.i * 2 + v.r)
                tail_xnT(v, m1)
                tail_choose_a(v)
                tail_dest_a(v)

            rounds(dve, RA, 0, 2, first_a, half_a, last_a,
                   before_loop=lambda: dve.wait_ge(s_x[1], 32))

            after()
            v_.tensor_scalar(nt_i[:, :], count0[0:1, :], float(P - 1), None, ALU.add)
            after()
            v_.tensor_scalar(nt_i[:, :], nt_i[:, :], 7, None, ALU.logical_shift_right)
            after()
            copy(nt_f[:, :], nt_i[:, :])
            after()
            v_.tensor_tensor_scan(ends[:, :], ones32[0:1, 0:E0], nt_f[:, :], 0.0, ALU.mult, ALU.add)
            after()
            jb = tilenum.unsqueeze(2).to_broadcast([1, TILES0, 7])
            v_.tensor_tensor(mp, jb, ends[:, 0:7].unsqueeze(1).to_broadcast([1, TILES0, 7]), ALU.is_ge)
            after()
            v_.tensor_reduce(etile[:, :], mp, AX.X, ALU.add)
            v_.tensor_tensor(mp2, mp, nt_f[:, 0:7].unsqueeze(1).to_broadcast([1, TILES0, 7]), ALU.mult)
            after()
            v_.tensor_reduce(stile[:, :], mp2, AX.X, ALU.add)
            after()
            v_.tensor_tensor(btile[:, :], tilenum, stile[:, :], ALU.subtract)
            after()
            v_.tensor_scalar(stile[:, :], etile[:, :], float(NTOK), None, ALU.mult)
            after()
            v_.scalar_tensor_tensor(base_i[:, :], btile[:, :], float(P), stile[:, :], ALU.mult, ALU.add)
            copy(etile_i[:, :], etile[:, :]).then_inc(s_map, 1)

            SCALE = float(D1) ** -0.5
            for a in range(2):
                rk = LAT if a else P
                if a:
                    after()
                copy(tmp[0:rk, :], cols[0:rk, a, 3:4].to_broadcast([rk, P])).then_inc(s_prep, 1)
                dve.wait_ge(s_prep_pe, a + 1)
                v_.tensor_scalar(bq[a][:, :], m0[:, 0:4], SCALE, None, ALU.mult)
                copy(bk[a][:, :], m0[:, 4:8])
                v_.tensor_tensor(b2c[a][:, :], m0[:, 8:12], b2c[a][:, :], ALU.add)
                copy(bv[a][:, :], m1[:, :]).then_inc(s_prep, 1)
                v_.tensor_scalar(wq[a][:, :], wq[a][:, :], cols[:, a, 0:1], SCALE, ALU.mult, ALU.mult)
                v_.tensor_scalar(wk[a][0:rk, :], wk[a][0:rk, :], cols[0:rk, a, 2:3], None, ALU.mult)
                v_.tensor_scalar(wv[a][0:rk, :], wv[a][0:rk, :], cols[0:rk, a, 2:3], None, ALU.mult)
                v_.tensor_scalar(li2[a][:, :], li2[a][:, :], cols[:, a, 4:5], None, ALU.mult)\
                    .then_inc(s_prep, 1)

            dve.wait_ge(s_ffnw, 64)

            def expert(i, k):
                return dve.value_load(etile_i[0:1, bass.ds(i * RING + k, 1)], min_val=0,
                                      max_val=E0 - 1)

            def tokens_T(u, k, q):
                dve.wait_ge(s_gt, u.count(1, 1))
                if positive(n := u.count(1, -1)):
                    dve.wait_ge(s_hps, n)
                copy(xgT[:, q, :], bank[q][:, 0:P]).then_inc(s_gT, 1)

            def hidden0(u, q, e):
                dve.wait_ge(s_hps, u.count(1, 1))
                if positive(n := u.count(1, -1)):
                    dve.wait_ge(s_htr, n)
                v_.tensor_tensor(h0[:, q, :], bank[2 + q][:, :],
                                 b1bc0[:, bass.ds(e, 1), :].rearrange("p o f -> p (o f)"), ALU.add)\
                    .then_inc(s_h, 1)

            def result0(u, k, e):
                dve.wait_ge(s_yps, u.count(1, 1))
                v_.tensor_tensor(yS[:, k, :], bank[6 + k % 2][:, 0:P],
                                 b2bc0[:, bass.ds(e, 1), :].rearrange("p o d -> p (o d)"), ALU.add)\
                    .then_inc(s_y, 1)

            def tile0(i, k, first):
                u = Unit(0, i, RING, k)
                if positive(n := i * 16):
                    dve.wait_ge(s_ysc[k], n)
                tokens_T(u, k, k % 2)
                hidden0(u, k % 2, expert(i, k))
                if not first or k > 0:
                    result0(u.shift(-1), (k - 1) % RING, expert(i, k - 1))

            ring_rounds(dve, TILES0, tile0,
                        lambda last: result0(Unit(0, last, RING, RING - 1), RING - 1,
                                             expert(last, RING - 1)))

            def head_ctx_stats(h):
                b = batch_unit(0, h)
                norm_stats(st_c, ctx_sb[:, b.i * 2 + b.r, :], s_cvar, CTX)

            def head_ctx(h):
                b = batch_unit(0, h)
                dve.wait_ge(s_crstd, b.count(1, 1))
                dve.wait_ge(s_ht, h.count(1, 0))
                dve.nop(nofuse=True)
                normalise(cS[:, :], ctx_sb[:, b.i * 2 + b.r, :], st_c, CTX).then_inc(s_c, 1)

            def head_stats(h):
                if (h.r % 4) // 2 == 0:
                    hb = batch_unit(0, h)
                    s, b = hb.r % 2, hb.i * 2 + hb.r
                    dve.wait_ge(s_y0[s], hb.i * 16 + 16 * (hb.r // 2) + 16)
                    v_.tensor_tensor(xres[:, b, :], xres[:, b, :], yb[:, s, :], ALU.add)\
                        .then_inc(s_x2, 1)
                    after()
                    norm_stats(st_h, xres[:, b, :], s_hvar, a=1.0 + EPS, c=EPS * EPS)
                else:
                    norm_stats(st_h, xp[:, :], s_hvar)

            def head_z(h):
                l = Unit(0, h.i, 4, h.r)
                a = (h.r % 4) // 2
                s = h.r % 2
                hb = batch_unit(0, h)
                src = xp[:, :] if a else xres[:, hb.i * 2 + hb.r, :]
                dve.wait_ge(s_hrstd, h.count(1, 1))
                v_.scalar_tensor_tensor(tmp[:, :], src, st_h[:, 6:7], g_ln[a][:, :],
                                        ALU.subtract, ALU.mult)
                after()
                if positive(n := l.count(1, -1)):
                    dve.wait_ge(s_ss, n)
                v_.scalar_tensor_tensor(xx[:, s, :], tmp[:, :], st_h[:, 9:10], b_ln[a][:, :],
                                        ALU.mult, ALU.add).then_inc(s_xx, 1)
                after()
                norm_stats(st_x, xx[:, s, :], s_xvar)

            def head_z2(h):
                l = Unit(0, h.i, 4, h.r)
                s = h.r % 2
                dve.wait_ge(s_xrstd, l.count(1, 1))
                dve.wait_ge(s_ht, h.count(1, 0))
                normalise(zS[:, :], xx[:, s, :], st_x).then_inc(s_z, 1)

            def head_t(h):
                dve.wait_ge(s_ht, h.count(1, 1))
                if (h.r % 4) // 2:
                    copy(cT[:, :], m0[0:LAT, P:P + CTX])
                copy(zT[:, :], m0[:, 0:P]).then_inc(s_zT, 1)

            def head_qkv(h):
                l = Unit(0, h.i, 4, h.r)
                a = (h.r % 4) // 2
                s = h.r % 2
                T = CTX if a else TOK
                dve.wait_ge(s_qps, h.count(1, 1))
                v_.tensor_tensor(qT[:, s, :].rearrange("p (c t) -> p c t", c=4),
                                 m1[:, :].rearrange("p (c t) -> p c t", c=4), bcast(bq[a][:, :], TOK),
                                 ALU.add).then_inc(s_q, 1)
                dve.wait_ge(s_kps, l.count(1, 1))
                v_.tensor_tensor(kT[:, s, 0:4 * T].rearrange("p (c t) -> p c t", c=4),
                                 m0[:, 0:4 * T].rearrange("p (c t) -> p c t", c=4),
                                 bcast(bk[a][:, :], T), ALU.add).then_inc(s_k, 1)
                dve.wait_ge(s_vps, l.count(1, 1))
                v_.tensor_tensor(vS[0:T, s, :], m1[0:T, :], bv[a][0:T, :], ALU.add).then_inc(s_v, 1)

            def tail_xo(v):
                l = Unit(0, v.i, 4, v.r)
                s = v.r % 2
                dve.wait_ge(s_li1, v.count(1, 1))
                dve.wait_ge(s_xxb, l.count(1, 1))
                v_.tensor_tensor(xo[:, :], m0[:, 0:P], xxb[:, s, :], ALU.add).then_inc(s_xo, 1)
                after()
                norm_stats(st_3, xo[:, :], s_3var)

            def tail_z3(v):
                dve.wait_ge(s_3rstd, Unit(0, v.i, 4, v.r).count(1, 1))
                normalise(z3[:, :], xo[:, :], st_3).then_inc(s_z3, 1)

            def tail_z3T(v):
                dve.wait_ge(s_z3t, Unit(0, v.i, 4, v.r).count(1, 1))
                copy(z3T[:, :], m1[:, 0:P]).then_inc(s_z3T, 1)

            def tail_sum(v):
                l = Unit(0, v.i, 4, v.r)
                vb = batch_unit(0, v)
                dve.wait_ge(s_ss, l.count(1, 1))
                dve.wait_ge(s_li3, l.count(1, 1))
                dst = xres[:, vb.i * 2 + vb.r, :] if (v.r % 4) // 2 else xp[:, :]
                v_.tensor_tensor(dst, m1[:, 0:P], ss[:, :], ALU.add)
                after()

            def tail_choose(v):
                vb = batch_unit(NB, v)
                dve.wait_ge(s_lgps, vb.count(1, 1))
                copy(lg[:, :], m1[:, 0:E1])
                after()
                v_.max(out=v8[:, :], in_=lg[:, :])
                after()
                v_.tensor_scalar(nv0[:, :], v8[:, 0:1], -1.0, None, ALU.mult).then_inc(s_v8, 1)
                v_.max_index(i8[:, :], v8[:, :], lg[:, :])
                after()
                copy(i8f[:, :], i8[:, 0:TOPK])
                after()
                v_.tensor_tensor(oh4[:, :, :], iota64.unsqueeze(1).to_broadcast([P, TOPK, E1]),
                                 i8f[:, :].unsqueeze(2).to_broadcast([P, TOPK, E1]), ALU.is_equal)
                after()
                v_.tensor_reduce(mask_f[:, :], oh4[:, :, :].rearrange("p k e -> p e k"), AX.X, ALU.add)
                after()
                copy(mask_b[:, :], mask_f[:, :]).then_inc(s_mask, 1)

            def tail_dest(v):
                vb = batch_unit(NB, v)
                s, b = vb.r % 2, vb.i * 2 + vb.r
                dve.wait_ge(s_el, batch_unit(0, v).count(1, 1))
                v_.reciprocal(rsum[:, :], esum[:, :])
                dve.wait_ge(s_cum, vb.count(1, 1))
                v_.tensor_tensor(pos[:, :], m0[:, 0:E1], count1[:, :], ALU.add)
                after()
                v_.tensor_tensor(count1[:, :], m0[:, E1:2 * E1], count1[:, :], ALU.add)\
                    .then_inc(s_cumr, 1)
                v_.scalar_tensor_tensor(posw[:, :], pos[:, :], float(E1), iota64, ALU.mult, ALU.add)
                v_.scalar_tensor_tensor(over[:, :], pos[:, :], float(CAP), mask_f[:, :],
                                        ALU.is_ge, ALU.mult)
                after()
                v_.tensor_tensor(oh4s[:, :, :], oh4[:, :, :],
                                 posw[:, :].unsqueeze(1).to_broadcast([P, TOPK, E1]), ALU.mult)
                v_.scalar_tensor_tensor(pover[:, b, :], expl[:, :], rsum[:, :], over[:, :],
                                        ALU.mult, ALU.mult)
                after()
                v_.tensor_reduce(dest_f[:, :], oh4s[:, :, :], AX.X, ALU.add)
                after()
                v_.tensor_scalar(pay_i[:, s, :, 0], pay_i[:, s, :, 0], 2.0 * P, None, ALU.add)
                v_.tensor_scalar(pay[:, s, :, 1], e4[:, :], rsum[:, :], None, ALU.mult)
                copy(dest[:, s, :], dest_f[:, :])\
                    .then_inc(s_dest, 1)

            def slots_free(u):
                dve.wait_ge(s_xnd[u.r % 2], u.i * 16 + 16 * (NB // 2))
                if positive(n := u.i * 64):
                    dve.wait_ge(s_sc1[u.r % 2], n)

            def route(v):
                vb = batch_unit(NB, v)
                tail_xn(vb, vb.i * 2 + vb.r)
                tail_xnT(vb, m0)
                tail_choose(v)
                tail_dest(v)

            def half_b(u, r, tail, head):
                T = CTX if r >= 2 else TOK
                v, h = u.shift(-1), u.shift(1)
                second = r in (1, 2)
                if head and second:
                    head_ctx_stats(h)
                maxima(u, 0, T)
                maxima(u, 1, T)
                if tail:
                    tail_xo(v)
                if head and second:
                    head_ctx(h)
                if head and not second:
                    head_stats(h)
                maxima(u, 2, T)
                if tail:
                    tail_z3(v)
                    tail_z3T(v)
                pt_odd(u, 1, T)
                maxima(u, 3, T)
                if head and not second:
                    head_z(h)
                    head_z2(h)
                pt_odd(u, 3, T)
                if tail:
                    tail_sum(v)
                    if not second:
                        norm_stats(st_n, xres[:, batch_unit(0, v).i * 2 + batch_unit(0, v).r, :],
                                   s_nvar)
                if head and second:
                    head_stats(h)
                finish_core(u, 512)
                if tail and not second:
                    route(v)
                if r >= 2:
                    slots_free(u)
                if head:
                    if second:
                        head_z(h)
                        head_z2(h)
                    head_t(h)
                    head_qkv(h)

            def first_b(h):
                head_stats(h)
                head_z(h)
                head_z2(h)
                head_t(h)
                head_qkv(h)

            def last_b(v):
                tail_xo(v)
                tail_z3(v)
                tail_z3T(v)
                tail_sum(v)
                norm_stats(st_n, xres[:, batch_unit(0, v).i * 2 + batch_unit(0, v).r, :], s_nvar)
                route(v)

            rounds(dve, RB, NB, 4, first_b, half_b, last_b)

            dve.wait_ge(s_l1, 16)
            v_.memset(list1[:, E1:E1 + 2, :], 0.0)
            after()

            def indices(i, k):
                k, i = k % RING, i + k // RING
                one = bass.ds(i * RING + k, 1)
                copy(wcol[:, k:k + 1], list1[:, one, 1])
                v_.tensor_scalar(ids[:, k:k + 1], list1_i[:, one, 0], NTOK - 1, None,
                                 ALU.bitwise_and).then_inc(s_idx, 1)

            def gate(u, q):
                dve.wait_ge(s_sil, Unit(0, u.i, RING, u.r).count(1, 1))
                dve.wait_ge(s_htr, u.count(1, -1))
                v_.tensor_tensor(glu[:, q, q * I1:(q + 1) * I1], bank[2 + q][:, I1:2 * I1], silu[:, q, 0:I1],
                                 ALU.mult).then_inc(s_h, 1)

            def gate_T(u, q):
                dve.wait_ge(s_htr, u.count(1, 1))
                dve.wait_ge(s_yps, u.count(1, -1))
                copy(h0T[:, q, 0:P], bank[4 + q][:, 0:P]).then_inc(s_hT, 1)

            def result1(u, k):
                dve.wait_ge(s_yps, u.count(1, 1))
                dve.wait_ge(s_ysc[k], Unit(u.base, u.i, RING, u.r - k).count(4))
                dve.nop(nofuse=True)
                copy(idr[:, k:k + 1], list1_i[:, bass.ds(u.i * RING + u.r, 1), 0])
                v_.tensor_scalar(yS[:, k, :], bank[6 + k % 2][:, 0:P], wcol[:, k:k + 1], None,
                                 ALU.mult).then_inc(s_y, 1)

            def tile1(i, k, first):
                u = Unit(TILES0, i, RING, k)
                p = u.shift(-1)
                tokens_T(u, k, k % 2)
                if not first or k > 0:
                    gate_T(p, (k - 1) % 2)
                gate(u, k % 2)
                if not first or k > 0:
                    result1(p, (k - 1) % RING)
                indices(i, k + 2)

            def end1(last):
                u = Unit(TILES0, last, RING, RING - 1)
                gate_T(u, 1)
                result1(u, RING - 1)

            for q in range(2):
                v_.memset(glu[:, q, (1 - q) * I1:(2 - q) * I1], 0.0)
            for k in range(2):
                indices(0, k)
            ring_rounds(dve, E1, tile1, end1)

            def step_c(i, k):
                u = Unit(0, i, RING, k)
                q = k % 2
                dve.wait_ge(s_ov, u.count(1, 1))
                v_.tensor_tensor(acc[:, k, :],
                                 xres[:, bass.ds(i * RING + k, 1), :].rearrange("p o d -> p (o d)"),
                                 bank[2 + q][:, 0:P], ALU.add).then_inc(s_acc, 1)
                dve.wait_ge(s_cs, u.count(1, 1))
                v_.tensor_tensor(acc2[:, k, :], csum2[:, q, 0:P], csum2[:, q, P:2 * P], ALU.add)
                after()
                if positive(n := i * 16):
                    dve.wait_ge(s_out[k], n)
                v_.tensor_tensor(outS[:, k, :], acc[:, k, :], acc2[:, k, :], ALU.add)\
                    .then_inc(s_fin, 1)

            for k in range(RING):
                step_c(0, k)
            with dve.Fori(1, NB // RING) as i:
                for k in range(RING):
                    step_c(i, k)


CST_WIDTH = 494 + 80
CSTI_WIDTH = 256 + 2 + 8


def constants(np, NB):
    ntok = NB * TOK
    c = np.zeros((P, CST_WIDTH), np.float32)
    p = np.arange(P)
    c[:, 0:128] = np.eye(P)
    c[:, 128:256] = p[:, None] < p[None, :]
    for g in range(NG):
        c[:, 256 + 32 * g + 8 * g:256 + 32 * g + 8 * g + 8] = 1.0
    c[:, 384:416] = 1.0
    c[:, 416:480] = np.arange(E1)
    c[:, 480:488] = np.arange(E0) * ntok
    c[:, 488:492] = (p[:, None] // D0) % 4 == np.arange(4)
    c[:, 493] = -0.5
    c[:, 494:574] = np.arange(80)
    n = np.zeros((P, CSTI_WIDTH), np.int32)
    n[:, 0:128] = ntok + np.arange(P)
    n[:, 128:256:2] = (TOPK * ntok + p)[:, None]
    for s in range(2):
        n[:, 256 + s] = p + TOK * s - 2 * TOK
        for k in range(TOPK):
            n[:, 258 + 4 * s + k] = k * ntok + p + TOK * s - 2 * TOK
    return c, n


def layouts(np, a):
    c = np.ascontiguousarray
    o = {"x": a["x"], "ctx": a["ctx_512"]}
    NB = a["x"].shape[0]
    o["cst"], o["cst_i"] = constants(np, NB)
    o["wqT0"] = c(a["L0_xattn_Wq"].T)
    o["wkvT0"] = c(a["L0_xattn_Wkv"].T)
    o["woT0"] = c(a["L0_xattn_Wo"].T.reshape(4, 4, D0, P).transpose(1, 0, 2, 3).reshape(P, P))
    o["wrT0"] = c(a["L0_ffn_Wr"].T)
    o["br0"] = a["L0_ffn_br"]
    o["w1T0"] = c(a["L0_ffn_W1"].transpose(2, 0, 1))
    o["w2T0"] = c(a["L0_ffn_W2"].reshape(E0, P, 4, P).transpose(3, 0, 2, 1))
    o["b10"] = a["L0_ffn_b1"]
    o["b20"] = a["L0_ffn_b2"]
    for k in range(2):
        m = f"L1_xattn_a{k + 1}_"
        for n in ("wq", "wk", "wv"):
            w = a[m + n]
            o[f"{n}{k}"] = c(w.transpose(1, 0, 2).reshape(w.shape[1], -1))
        o[f"li1{k}"] = c(a[m + "li1_w"].reshape(4, 4, D1, P).transpose(0, 2, 1, 3).reshape(P, 4 * P))
        o[f"li2{k}"] = a[m + "li2_w"]
        o[f"li3{k}"] = c(a[m + "li3_w"].reshape(4, P, P).transpose(1, 0, 2).reshape(P, 4 * P))
        o[f"b2c{k}"] = c(a[m + "li2_b"].reshape(4, P).T)
        o[f"li1b{k}"] = a[m + "li1_b"]
        o[f"li3b{k}"] = a[m + "li3_b"]
        o[f"g_ln{k}"] = a[f"L1_xattn_ln{k + 1}_g"]
        o[f"b_ln{k}"] = a[f"L1_xattn_ln{k + 1}_b"]
        for n in ("lnx", "lny", "ln3"):
            for x in "gb":
                o[f"{n}{x}{k}"] = a[f"{m}{n}_{x}"].reshape(-1, 1)
    o["router"] = a["L1_ffn_router_w"]
    o["w1_1"] = c(a["L1_ffn_w1"].transpose(1, 0, 2))
    o["w2_1"] = c(a["L1_ffn_w2"].reshape(E1 // 2, 2 * I1, P).transpose(1, 0, 2))
    return o


def kernel(**inputs):
    import numpy as np
    import concourse.bacc as bacc
    from concourse.bass_utils import run_bass_kernel_spmd

    a = {k: np.asarray(v) for k, v in inputs.items()}
    arrays = {f"in_{k}": np.ascontiguousarray(v) for k, v in layouts(np, a).items()}
    NB = a["x"].shape[0]
    nc = bacc.Bacc("TRN2", target_bir_lowering=False, num_devices=1)
    t = {k[3:]: nc.dram_tensor(k, v.shape, mybir.dt.from_np(v.dtype), kind="ExternalInput").ap()
         for k, v in arrays.items()}
    out = nc.dram_tensor("out", (NB * TOK, P), F32, kind="ExternalOutput").ap()
    build_program(nc, t, out, NB)
    r = run_bass_kernel_spmd(nc, [arrays], core_ids=[0])
    return r.results[0]["out"].reshape(NB, TOK, P)
```

```python
import concourse.bass as bass
from concourse import mybir
from contextlib import ExitStack

F32 = mybir.dt.float32
BF16 = mybir.dt.bfloat16
I32 = mybir.dt.int32
U32 = mybir.dt.uint32
ALU = mybir.AluOpType
ACT = mybir.ActivationFunctionType
AX = mybir.AxisListType

P = 128
TOK = 128
CTX = 120
LAT = 64
HEADS = 16
NG = 4
D0 = 8
D1 = 32
E0, FF0 = 8, 512
E1, TOPK, CAP, I1 = 64, 4, 128, 64
EPS = 1e-5


def positive(n):
    return not isinstance(n, int) or n > 0


class Unit:

    def __init__(self, base, i, per, r):
        self.base, self.i, self.per, self.r = base, i, per, r

    def count(self, each, k=0):
        return self.i * (self.per * each) + ((self.base + self.r) * each + k)

    def shift(self, d):
        return Unit(self.base, self.i, self.per, self.r + d)


def build_program(nc, t, out, NB=64):
    NTOK = NB * TOK
    TILES0 = NB + E0
    PAD0 = NTOK
    SLOTS0 = E0 * NTOK + TILES0 * P
    SLOTS1 = E1 * CAP
    CROWS = TOPK * NTOK

    xn0_d = nc.dram_tensor("xn0_d", (NTOK + P, P), F32).ap()
    y0_d = nc.dram_tensor("y0_d", (NTOK, P), F32).ap()
    list0_d = nc.dram_tensor("list0_d", (SLOTS0, 1), I32).ap()
    xn1_d = nc.dram_tensor("xn1_d", (NTOK, P), F32).ap()
    list1_d = nc.dram_tensor("list1_d", (SLOTS1, 2), F32).ap()
    c_d = nc.dram_tensor("c_d", (CROWS, P), F32).ap()
    y127_d = nc.dram_tensor("y127_d", (E1, P), F32).ap()

    ctx = ExitStack()
    with ctx:
        def sb(name, shape, dt=F32):
            return ctx.enter_context(nc.sbuf_tensor(name, shape, dt))

        def sem(name):
            return ctx.enter_context(nc.semaphore(name))

        xres = sb("xres", [P, NB, P])
        ctx_sb = sb("ctx_sb", [CTX, NB, LAT])
        pover = sb("pover", [P, NB, E1])
        big = sb("big", [P, 12288])
        w1T0 = big[:, 0:4096].rearrange("p (e f) -> p e f", e=E0)
        w2T0 = big[:, 4096:8192].rearrange("p (e c d) -> p e c d", e=E0, c=4)
        b1bc0 = big[:, 8192:12288].rearrange("p (e f) -> p e f", e=E0)
        w1_1 = big[:, 0:8192].rearrange("p (e f) -> p e f", e=E1)
        w2_1 = big[:, 8192:12288].rearrange("p (e h) -> p e h", e=E1 // 2)

        cst = sb("cst", [P, CST_WIDTH])
        cst_i = sb("cst_i", [P, CSTI_WIDTH], I32)
        ident = cst[:, 0:128]
        ltri_f = cst[:, 128:256]
        ones_h = cst[:, 256:384].rearrange("p (g c) -> p g c", g=NG)
        ones32 = cst[:, 384:416]
        iota64 = cst[:, 416:480]
        slot0 = cst[:, 480:488]
        kmask = cst[:, 488:492]
        neghalf = cst[:, 493:494]
        tilenum = cst[0:1, 494:494 + TILES0]
        padlist0 = cst_i[:, 0:128]
        padlist1 = cst_i[:, 128:256]
        tokid = cst_i[:, 256:258]
        ltri = sb("ltri", [P, P], BF16)
        onesb = sb("onesb", [P, P], BF16)
        zeros = sb("zeros", [P, P])

        wqT0 = sb("wqT0", [P, P])
        wkvT0 = sb("wkvT0", [LAT, 2 * P])
        woT0 = sb("woT0", [P, P])
        wrT0 = sb("wrT0", [P, E0])
        br0 = sb("br0", [P, E0])
        rw1 = sb("rw1", [P, E1])
        wq, wk, wv, li1, li2, li3, bv = ([sb(f"{n}{a}", [P, 512]) for a in (1, 2)]
                                         for n in ("wq", "wk", "wv", "li1", "li2", "li3", "bv"))
        bq, bk, b2c = ([sb(f"{n}{a}", [P, 4]) for a in (1, 2)] for n in ("bq", "bk", "b2c"))
        li1b, li3b, g_ln, b_ln = ([sb(f"{n}{a}", [P, P]) for a in (1, 2)]
                                  for n in ("li1b", "li3b", "g_ln", "b_ln"))
        cols = sb("cols", [P, 2, 6])

        qT = sb("qT", [P, 2, 512])
        kT = sb("kT", [P, 512])
        kbd = sb("kbd", [P, NG, 512])
        vS = sb("vS", [P, 2, 512])
        nmax = sb("nmax", [P, 2, 4])
        prob = sb("prob", [P, 2, 512])
        pT = sb("pT", [P, 2, 512])
        pTm = sb("pTm", [P, 2, 512])
        den = sb("den", [P, 2, HEADS])
        rd = sb("rd", [P, HEADS])
        rdx = sb("rdx", [P, 512])
        rS = sb("rS", [P, 512])
        oT = sb("oT", [P, 2, 512])

        zS = sb("zS", [P, P])
        zT = sb("zT", [P, P])
        cS = sb("cS", [CTX, LAT])
        cT = sb("cT", [LAT, CTX])
        yb = sb("yb", [P, 2, P])
        tmp = sb("tmp", [P, P])
        xx = sb("xx", [P, P])
        shared = sb("shared", [P, 1024])
        xxb = shared[:, 0:512].rearrange("p (u d) -> p u d", d=P)
        hT = shared[:, 512:1024]
        b2bc0 = shared[:, :].rearrange("p (e d) -> p e d", e=E0)
        xo = sb("xo", [P, P])
        ss = sb("ss", [P, P])
        ssa = sb("ssa", [P, P])
        ssb = sb("ssb", [P, P])
        xp = sb("xp", [P, 2, P])
        z3 = sb("z3", [P, P])
        z3T = sb("z3T", [P, P])
        xnS = sb("xnS", [P, 2, P])
        xnT = sb("xnT", [P, P])
        st_h, st_x, st_c, st_3, st_n = (sb(n, [P, 10]) for n in
                                        ("st_h", "st_x", "st_c", "st_3", "st_n"))
        lg = sb("lg", [P, E1])
        v8 = sb("v8", [P, 8])
        i8 = sb("i8", [P, 8], U32)
        i8f = sb("i8f", [P, 4])
        nv0 = sb("nv0", [P, 1])
        expl = sb("expl", [P, E1])
        esum = sb("esum", [P, 1])
        rsum = sb("rsum", [P, 1])
        e4 = sb("e4", [P, 4])
        oh4 = sb("oh4", [P, TOPK, E1])
        oh4s = sb("oh4s", [P, TOPK, E1])
        mask_b = sb("mask_b", [P, E1], BF16)
        mask_f = sb("mask_f", [P, E1])
        count0 = sb("count0", [P, E0])
        count1 = sb("count1", [P, E1])
        pos = sb("pos", [P, E1])
        posw = sb("posw", [P, E1])
        over = sb("over", [P, E1])
        dest_f = sb("dest_f", [P, 4])
        dest = sb("dest", [P, 2, 4], U32)
        pay = sb("pay", [P, 2, TOPK, 2])
        pay_i = pay[:, :, :, :].bitcast(I32)

        RING = 4
        ids = sb("ids", [P, RING], I32)
        idr = sb("idr", [P, RING], I32)
        wcol = sb("wcol", [P, RING])
        xg = qT[:, :, :].rearrange("p a (b d) -> p (a b) d", d=P)[:, 0:RING, :]
        yS = qT[:, :, :].rearrange("p a (b d) -> p (a b) d", d=P)[:, RING:2 * RING, :]
        xgT = pTm[:, 0, :].rearrange("p (b d) -> p b d", d=P)[:, 0:2, :]
        silu = pTm[:, 1, :].rearrange("p (b d) -> p b d", d=P)[:, 0:2, :]
        glu = pTm[:, 1, :].rearrange("p (b d) -> p b d", d=P)[:, 2:4, :]
        h0, h0T = prob, pT
        ylast = kT[:, :].rearrange("p (b d) -> p b d", d=P)
        mp = oT[0:1, :, :].rearrange("p a b -> p (a b)")[:, 0:TILES0 * 7].rearrange("p (j e) -> p j e", e=7)
        mp2 = vS[0:1, :, :].rearrange("p a b -> p (a b)")[:, 0:TILES0 * 7].rearrange("p (j e) -> p j e", e=7)
        nt_i = sb("nt_i", [1, E0], I32)
        nt_f = sb("nt_f", [1, E0])
        ends = sb("ends", [1, E0])
        etile, stile, btile = (rS[0:1, at:at + TILES0] for at in (0, P, 2 * P))
        etile_i = sb("etile_i", [1, TILES0], I32)
        base_i = sb("base_i", [1, TILES0], I32)
        list1 = kbd[:, 0, 0:2 * (E1 + 2)].rearrange("p (e c) -> p e c", c=2)
        list1_i = list1.bitcast(I32)
        y127 = kbd[0:E1, 1, 0:P]
        cb = [vS[:, 0, :], vS[:, 1, :], oT[:, 0, :], oT[:, 1, :]]
        poS = pT[:, 0, :].rearrange("p (b d) -> p b d", d=P)
        poT = pT[:, 1, :].rearrange("p (b d) -> p b d", d=P)
        csum2 = prob
        acc = pTm[:, 0, :].rearrange("p (b d) -> p b d", d=P)
        acc2 = pTm[:, 1, :].rearrange("p (b d) -> p b d", d=P)
        outS = kT[:, :].rearrange("p (b d) -> p b d", d=P)

        bank = [ctx.enter_context(nc.psum_tensor(f"bank{i}", [P, 512], F32)) for i in range(8)]
        sbank, tbank = bank[0:2], bank[2:4]
        obank, dbank = bank[4], bank[5]
        m0, m1 = bank[6], bank[7]

        s_const = sem("s_const")
        s_load = sem("s_load")
        s_x = [sem("s_x_first"), sem("s_x_rest")]
        s_ffnw = sem("s_ffnw")
        s_made = sem("s_made")
        s_init = sem("s_init")
        s_c0 = sem("s_c0")
        s_prep = sem("s_prep")
        s_prep_pe = sem("s_prep_pe")
        s_q, s_k, s_v = sem("s_q"), sem("s_k"), sem("s_v")
        s_kd = [sem(f"s_kd{g}") for g in range(NG)]
        s_s = sem("s_s")
        s_max = sem("s_max")
        s_exp = sem("s_exp")
        s_tr = sem("s_tr")
        s_pt = [sem("s_pt_even"), sem("s_pt_odd")]
        s_ptm = sem("s_ptm")
        s_pv = sem("s_pv")
        s_rd = sem("s_rd")
        s_r = sem("s_r")
        s_rs = sem("s_rs")
        s_oT = sem("s_oT")
        s_hvar, s_hrstd = sem("s_hvar"), sem("s_hrstd")
        s_xvar, s_xrstd = sem("s_xvar"), sem("s_xrstd")
        s_cvar, s_crstd = sem("s_cvar"), sem("s_crstd")
        s_z, s_c = sem("s_z"), sem("s_c")
        s_ht = sem("s_ht")
        s_zT = sem("s_zT")
        s_qps, s_kps, s_vps = sem("s_qps"), sem("s_kps"), sem("s_vps")
        s_xxb = sem("s_xxb")
        s_y0 = [sem("s_y0_even"), sem("s_y0_odd")]
        s_x2 = sem("s_x2")
        s_li1 = sem("s_li1")
        s_xo = sem("s_xo")
        s_3var, s_3rstd = sem("s_3var"), sem("s_3rstd")
        s_z3, s_z3t, s_z3T = sem("s_z3"), sem("s_z3t"), sem("s_z3T")
        s_li2, s_gelu, s_li3 = sem("s_li2"), sem("s_gelu"), sem("s_li3")
        s_ss = sem("s_ss")
        s_sum = sem("s_sum")
        s_nvar, s_nrstd = sem("s_nvar"), sem("s_nrstd")
        s_xn, s_xnt, s_xnT = sem("s_xn"), sem("s_xnt"), sem("s_xnT")
        s_lgps = sem("s_lgps")
        s_lg = sem("s_lg")
        s_v8 = sem("s_v8")
        s_el = sem("s_el")
        s_mask = sem("s_mask")
        s_cum = sem("s_cum")
        s_pos = sem("s_pos")
        s_cumr = sem("s_cumr")
        s_dest = sem("s_dest")
        s_xnd = [sem("s_xnd_even"), sem("s_xnd_odd")]
        s_sc = [sem("s_sc_even"), sem("s_sc_odd")]
        s_sc1 = [sem("s_sc1_even"), sem("s_sc1_odd")]
        s_map = sem("s_map")
        s_ids = [sem(f"s_ids{k}") for k in range(RING)]
        s_idx = sem("s_idx")
        s_g = [sem(f"s_g{k}") for k in range(RING)]
        s_gt, s_gT = sem("s_gt"), sem("s_gT")
        s_hps, s_h = sem("s_hps"), sem("s_h")
        s_htr, s_hT = sem("s_htr"), sem("s_hT")
        s_yps, s_y = sem("s_yps"), sem("s_y")
        s_ysc = [sem(f"s_ysc{k}") for k in range(RING)]
        s_w1 = sem("s_w1")
        s_l1 = sem("s_l1")
        s_sil = sem("s_sil")
        s_yl = sem("s_yl")
        s_y127d = sem("s_y127d")
        s_yld = [sem(f"s_yld{k}") for k in range(RING)]
        s_cld = [sem(f"s_cld{k}") for k in range(RING)]
        s_po, s_pot, s_poT = sem("s_po"), sem("s_pot"), sem("s_poT")
        s_ov, s_acc, s_cs, s_fin = sem("s_ov"), sem("s_acc"), sem("s_cs"), sem("s_fin")
        s_out = [sem(f"s_out{k}") for k in range(RING)]

        N_LOADS = 5 + 1 + 2 * 17
        FIRST = min(8, NB // 2)
        NINIT = -(-(SLOTS0 // P) // P) + 2

        class Work:

            def __init__(self, i, per, off, first, a, base):
                self.i, self.per, self.off, self.first, self.a, self.base = i, per, off, first, a, base
                self.slot, self.ring = off % 2, off % 4
                self.bs = first % 2
                self.batch = i * 2 + first
                self.T = CTX if a or not base else TOK
                self.rk = LAT if a or not base else P

            def n(self, each, k=0):
                return self.i * (self.per * each) + ((self.base + self.off) * each + k)

            def l(self, each, k=0):
                return self.i * (self.per * each) + (self.off * each + k)

            def b(self, each, k=0):
                return self.i * (2 * each) + (self.first * each + k)

            def gb(self, each, k=0):
                return self.i * (2 * each) + ((self.base + self.first) * each + k)

            def pair(self, each):
                return self.i * each + self.first // 2 * each

        NPAIR = NB // 2

        def pipeline_a(eng, half, before_loop=None):
            def fixed(p):
                return lambda d: Work(0, 2, p + d, p + d, 0, 0) if 0 <= p + d < NB else None
            for p in range(-4, 6):
                half(fixed(p))
            if before_loop:
                before_loop()
            with eng.Fori(3, NPAIR - 2) as i:
                for r in range(2):
                    half(lambda d: Work(i, 2, r + d, r + d, 0, 0))
            for p in range(NB - 4, NB + 4):
                half(fixed(p))

        def pipeline_b(eng, half):
            def seq(i, r):
                q, rr = divmod(r, 4)
                a = rr % 2
                return Work(i, 4, r - 2, 2 * q + rr // 2 - 2 * a, a, NB)

            def fixed(p):
                def at(d):
                    q = p + d
                    if 2 <= q < 2 * NB - 2:
                        return seq(0, q + 2)
                    ends = {-2: (0, 0, 0), 0: (1, 1, 0), 2 * NB - 1: (2 * NB - 2, NB - 2, 1),
                            2 * NB + 1: (2 * NB - 1, NB - 1, 1)}
                    return Work(0, 4, *ends[q], NB) if q in ends else None
                return at
            for p in range(-6, 10):
                half(fixed(p))
            with eng.Fori(3, NPAIR - 1) as i:
                for r in range(4):
                    half(lambda d: seq(i, r + d))
            for p in range(2 * NB - 6, 2 * NB + 7):
                half(fixed(p))

        def ring_rounds(eng, n, step, after):
            for k in range(RING):
                step(0, k, True)
            with eng.Fori(1, n // RING) as i:
                for k in range(RING):
                    step(i, k, False)
            after(n // RING - 1)

        block = ctx.enter_context(nc.Block())

        @block.sync
        def _(sp):
            x_v = t["x"].rearrange("b s d -> s b d")
            c_v = t["ctx"].rearrange("b s d -> s b d")
            sp.dma_start(cst[:, :], t["cst"]).then_inc(s_const, 16)
            sp.dma_start(cst_i[:, :], t["cst_i"]).then_inc(s_const, 16)
            sp.dma_start(xres[:, 0:FIRST, :], x_v[:, 0:FIRST, :]).then_inc(s_x[0], 16)
            sp.dma_start(ctx_sb[:, 0:FIRST, :], c_v[:, 0:FIRST, :]).then_inc(s_x[0], 16)
            for dst, name in ((wqT0, "wqT0"), (wkvT0, "wkvT0"), (woT0, "woT0"), (wrT0, "wrT0"),
                              (rw1, "router")):
                sp.dma_start(dst[:, :], t[name]).then_inc(s_load, 16)
            sp.dma_start(br0[:, :], t["br0"].partition_broadcast(P)).then_inc(s_load, 16)
            sp.dma_start(xres[:, FIRST:NB, :], x_v[:, FIRST:NB, :]).then_inc(s_x[1], 16)
            sp.dma_start(ctx_sb[:, FIRST:NB, :], c_v[:, FIRST:NB, :]).then_inc(s_x[1], 16)
            for a in range(2):
                for n, dst in (("wq", wq), ("wk", wk), ("wv", wv), ("li1", li1), ("li2", li2),
                               ("li3", li3), ("b2c", b2c)):
                    rows = LAT if (a == 1 and n in ("wk", "wv")) else P
                    sp.dma_start(dst[a][0:rows, :], t[f"{n}{a}"]).then_inc(s_load, 16)
                for n, dst in (("li1b", li1b), ("li3b", li3b), ("g_ln", g_ln), ("b_ln", b_ln)):
                    sp.dma_start(dst[a][:, :], t[f"{n}{a}"].partition_broadcast(P)).then_inc(s_load, 16)
                for k, n in enumerate(("lnxg", "lnxb", "lnyg", "lnyb", "ln3g", "ln3b")):
                    rows = LAT if (a == 1 and n.startswith("lny")) else P
                    sp.dma_start(cols[0:rows, a, k:k + 1], t[f"{n}{a}"]).then_inc(s_load, 16)
            sp.wait_ge(s_const, 32)
            sp.wait_ge(s_made, 2)
            rows = SLOTS0 // P
            list0_rows = list0_d.rearrange("(r q) o -> r (q o)", q=P)
            for at in range(0, rows, P):
                n = min(P, rows - at)
                sp.dma_start(list0_rows[at:at + n, :], padlist0[0:n, :]).then_inc(s_init, 16)
            list1_v = list1_d.rearrange("(p e) c -> p (e c)", e=E1)
            sp.dma_start(list1_v, padlist1[:, :].bitcast(F32)).then_inc(s_init, 16)
            sp.dma_start(xn0_d[NTOK:NTOK + P, :], zeros[:, :]).then_inc(s_init, 16)
            sp.dma_start(w1T0, t["w1T0"]).then_inc(s_ffnw, 16)
            sp.dma_start(w2T0, t["w2T0"]).then_inc(s_ffnw, 16)
            sp.dma_start(b1bc0, t["b10"].partition_broadcast(P)).then_inc(s_ffnw, 16)
            sp.dma_start(b2bc0, t["b20"].partition_broadcast(P)).then_inc(s_ffnw, 16)

            c_rows = c_d.rearrange("(n p a) d -> n p a d", p=P, a=4)
            zeros4 = zeros[:, :].unsqueeze(1).to_broadcast([P, 4, P])
            n_c = CROWS // (4 * P)

            def store_xn(v, dst):
                sp.wait_ge(s_xn, v.gb(1, 1))
                sp.nop(nofuse=True)
                sp.dma_start(dst[bass.ds(v.batch * P, P), :], xnS[:, v.bs, :])\
                    .then_inc(s_xnd[v.bs], 16)

            def spread_keys(h):
                w = 4 * h.T
                for g in range(NG):
                    if g == 0:
                        sp.wait_ge(s_k, h.n(1, 1))
                        sp.nop(nofuse=True)
                    if positive(n := h.n(4, g - 3)):
                        sp.wait_ge(s_s, n)
                        sp.nop(nofuse=True)
                    rows = slice(32 * g, 32 * g + 32)
                    sp.dma_start(kbd[rows, g, 0:w], kT[rows, 0:w]).then_inc(s_kd[g], 16)

            def half_a(at):
                if at(1):
                    spread_keys(at(1))
                if at(0):
                    sp.dma_start(c_rows[at(0).batch], zeros4).then_inc(s_c0, 16)
                if at(-2):
                    store_xn(at(-2), xn0_d)

            pipeline_a(sp, half_a)

            for s in range(2):
                sp.wait_ge(s_sc[s], 16 * (NB // 2))
            sp.wait_ge(s_map, 1)

            def tile_ids(i, k, first):
                at = sp.value_load(base_i[0:1, bass.ds(i * RING + k, 1)], min_val=0,
                                   max_val=SLOTS0 - P)
                if positive(n := i * 16):
                    sp.wait_ge(s_ysc[k], n)
                    sp.nop(nofuse=True)
                sp.dma_start(ids[:, k:k + 1], list0_d[bass.ds(at, P), :]).then_inc(s_ids[k], 16)

            ring_rounds(sp, TILES0, tile_ids, lambda last: None)

            for k in range(RING):
                sp.wait_ge(s_ysc[k], 16 * (TILES0 // RING))
            sp.wait_ge(s_y, TILES0)
            sp.dma_start(w1_1, t["w1_1"]).then_inc(s_w1, 16)
            sp.dma_start(w2_1, t["w2_1"]).then_inc(s_w1, 16)

            def half_b(at):
                y, t3 = at(4), at(-3)
                if y and y.a == 0:
                    if positive(n := y.b(1, -1)):
                        sp.wait_ge(s_x2, n)
                        sp.nop(nofuse=True)
                    sp.dma_start(yb[:, y.bs, :], y0_d[bass.ds(y.batch * P, P), :])\
                        .then_inc(s_y0[y.bs], 16)
                if at(1):
                    spread_keys(at(1))
                if t3 and t3.a:
                    store_xn(t3, xn1_d)

            pipeline_b(sp, half_b)

            for s in range(2):
                sp.wait_ge(s_sc1[s], 64 * (NB // 2))
            sp.dma_start(list1[:, 0:E1, :], list1_d.rearrange("(p e) c -> p e c", e=E1))\
                .then_inc(s_l1, 16)

            def store_last(i, k, first):
                sp.wait_ge(s_yl, i * RING + k + 1)
                sp.nop(nofuse=True)
                sp.dma_start(y127_d[bass.ds(i * RING + k, 1), :], ylast[127:128, k, :])\
                    .then_inc(s_yld[k], 16)

            ring_rounds(sp, E1, store_last, lambda last: None)
            for k in range(RING):
                sp.wait_ge(s_yld[k], 16 * (E1 // RING))
            sp.dma_start(y127[:, :], y127_d).then_inc(s_y127d, 16)

            for k in range(RING):
                sp.wait_ge(s_ysc[k], 16 * ((TILES0 + E1) // RING))
            c_v4 = c_d.rearrange("(k t) d -> t k d", k=TOPK)

            def load_c(i, k):
                if positive(n := (i * RING + k) - RING + 1):
                    sp.wait_ge(s_cs, n)
                    sp.nop(nofuse=True)
                sp.dma_start(cb[k].rearrange("p (k d) -> p k d", k=TOPK),
                             c_v4[bass.ds((i * RING + k) * P, P), :, :]).then_inc(s_cld[k], 16)

            def store_out(i, k):
                sp.wait_ge(s_fin, i * RING + k + 1)
                sp.nop(nofuse=True)
                sp.dma_start(out[bass.ds((i * RING + k) * P, P), :], outS[:, k, :])\
                    .then_inc(s_out[k], 16)

            for k in range(RING):
                load_c(0, k)
            with sp.Fori(0, NB // RING - 1) as i:
                for k in range(RING):
                    store_out(i, k)
                    load_c(i + 1, k)
            for k in range(RING):
                store_out(NB // RING - 1, k)
            for k in range(RING):
                sp.wait_ge(s_out[k], 16 * (NB // RING))
            sp.wait_ge(s_c0, 16 * n_c)
            for s in range(2):
                sp.wait_ge(s_xnd[s], 16 * NB)

        @block.tensor
        def _(pe):
            mm, tr = nc.tensor.matmul, nc.tensor.transpose

            def scores(u, g):
                s, T = u.slot, u.T
                if g == 0:
                    pe.wait_ge(s_q, u.n(1, 1))
                pe.wait_ge(s_kd[g], u.n(16, 16))
                if positive(n := u.n(4, g - 1)):
                    pe.wait_ge(s_exp, n)
                o = sbank[g % 2]
                if u.base == 0:
                    last = mm(o[:, 0:4 * T], qT[:, s, 0:P], kbd[:, g, 0:4 * T],
                              start=True, stop=True)
                else:
                    for c in range(4):
                        last = mm(o[:, c * T:(c + 1) * T], qT[:, s, c * P:(c + 1) * P],
                                  kbd[:, g, c * T:(c + 1) * T], start=True, stop=True)
                last.then_inc(s_s, 1)

            def scores_ahead(u, h, g):
                if g < 2 and u:
                    scores(u, g + 2)
                if g >= 2 and h:
                    scores(h, g - 2)

            def transposes(u, g):
                T = u.T
                pe.wait_ge(s_exp, u.n(4, g + 1))
                if positive(n := u.n(2, g // 2)):
                    pe.wait_ge(s_pt[g % 2], n)
                for c in range(4):
                    last = tr(tbank[g % 2][0:T, c * P:(c + 1) * P],
                              prob[:, g % 2, c * T:(c + 1) * T], ident)
                last.then_inc(s_tr, 1)

            def values(u, g):
                s, T = u.slot, u.T
                pe.wait_ge(s_pt[g % 2], u.n(2, g // 2 + 1))
                if g == 0:
                    pe.wait_ge(s_v, u.n(1, 1))
                    if positive(n := u.n(1, 0)):
                        pe.wait_ge(s_oT, n)
                if u.base == 0:
                    for j in range(4):
                        last = mm(obank[32 * j:32 * j + 32, 0:P],
                                  vS[0:T, s, (4 * g + j) * 32:(4 * g + j + 1) * 32],
                                  pT[0:T, g % 2, j * P:(j + 1) * P], start=(g == 0), stop=(g == 3))
                else:
                    w = pT
                    if u.a == 0:
                        w = pTm
                        pe.wait_ge(s_ptm, u.b(4, g + 1))
                    for c in range(4):
                        last = mm(obank[32 * c:32 * c + 32, g * P:(g + 1) * P],
                                  vS[0:T, s, (4 * c + g) * 32:(4 * c + g + 1) * 32],
                                  w[0:T, g % 2, c * P:(c + 1) * P], start=True, stop=True)
                last.then_inc(s_pv, 1)

            def spread(u):
                pe.wait_ge(s_rd, u.n(1, 1))
                if positive(n := u.n(1, 0)):
                    pe.wait_ge(s_rs, n)
                for g in range(1 if u.base == 0 else 4):
                    w = slice(g * P, (g + 1) * P)
                    last = mm(dbank[:, w], rdx[:, w], ident, start=True, stop=True)
                last.then_inc(s_r, 1)

            def router_transpose(v, b):
                pe.wait_ge(s_xn, v.gb(1, 1))
                tr(b[:, 0:P], xnS[:, v.bs, :], ident).then_inc(s_xnt, 1)

            def router_logits(v, b, w, n):
                pe.wait_ge(s_xnT, v.gb(1, 1))
                mm(b[:, 0:n], xnT[:, :], w[:, :], start=True, stop=True).then_inc(s_lgps, 1)

            def router_counts(v, b, n):
                pe.wait_ge(s_mask, v.gb(1, 1))
                mm(b[:, 0:n], ltri[:, :], mask_b[:, 0:n], start=True, stop=True)
                mm(b[:, n:2 * n], onesb[:, :], mask_b[:, 0:n], start=True, stop=True)\
                    .then_inc(s_cum, 1)

            pe.wait_ge(s_const, 32)
            pe.wait_ge(s_load, 16 * N_LOADS)
            pe.wait_ge(s_made, 4)

            def inputs_T(h):
                if h.base == 0:
                    pe.wait_ge(s_c, h.n(1, 1))
                elif h.a:
                    pe.wait_ge(s_c, h.gb(1, 1))
                pe.wait_ge(s_z, h.n(1, 1))
                last = tr(m0[:, 0:P], zS[:, :], ident)
                if h.base == 0 or h.a:
                    last = tr(m0[0:LAT, P:P + CTX], cS[:, :], ident[0:CTX, 0:CTX])
                last.then_inc(s_ht, 1)

            def half_a(at):
                u, t, t2, t3, h, h2 = at(0), at(-1), at(-2), at(-3), at(1), at(2)
                scores_ahead(u, h, 0)
                if u:
                    transposes(u, 0)
                if h:
                    pe.wait_ge(s_zT, h.n(1, 1))
                    mm(m1[:, 0:P], wqT0[:, :], zT[:, :], start=True, stop=True)
                    mm(m1[:, P:P + CTX], wkvT0[:, 0:P], cT[:, :], start=True, stop=True)
                    mm(m1[0:CTX, 256:384], cT[:, :], wkvT0[:, P:2 * P], start=True, stop=True)\
                        .then_inc(s_qps, 1)
                if t:
                    if t3:
                        pe.wait_ge(s_lg, t3.n(1, 1))
                    spread(t)
                    values(t, 3)

                scores_ahead(u, h, 1)
                if u:
                    transposes(u, 1)
                if t2:
                    if t:
                        pe.wait_ge(s_rs, t.n(1, 1))
                    router_transpose(t2, dbank)
                if u:
                    values(u, 0)

                scores_ahead(u, h, 2)
                if u:
                    transposes(u, 2)
                if t:
                    pe.wait_ge(s_oT, t.n(1, 1))
                    if h:
                        pe.wait_ge(s_zT, h.n(1, 1))
                    mm(m0[:, 0:P], oT[:, t.slot, 0:P], woT0[:, :], start=True, stop=True)\
                        .then_inc(s_li1, 1)
                if u:
                    values(u, 1)
                if t3:
                    if h:
                        pe.wait_ge(s_v, h.n(1, 1))
                    router_counts(t3, m1, E0)

                scores_ahead(u, h, 3)
                if t2:
                    router_logits(t2, dbank, wrT0, E0)
                if u:
                    transposes(u, 3)
                if h2:
                    if t:
                        pe.wait_ge(s_nvar, t.n(1, 1))
                    inputs_T(h2)
                if u:
                    values(u, 2)
                if t3:
                    pe.wait_ge(s_cumr, t3.n(1, 1))

            pipeline_a(pe, half_a)

            for a in range(2):
                rk = LAT if a else P
                pe.wait_ge(s_prep, 3 * a + 1)
                for c in range(4):
                    w = slice(c * P, (c + 1) * P)
                    mm(m0[:, c:c + 1], wq[a][:, w], cols[:, a, 1:2], start=True, stop=True)
                    mm(m0[:, 4 + c:5 + c], wk[a][0:rk, w], cols[0:rk, a, 3:4], start=True, stop=True)
                    mm(m0[:, 8 + c:9 + c], li2[a][:, w], cols[:, a, 5:6], start=True, stop=True)
                mm(m1[:, :], tmp[0:rk, :], wv[a][0:rk, :], start=True, stop=True).then_inc(s_prep_pe, 1)

            pe.wait_ge(s_map, 1)
            pe.wait_ge(s_ffnw, 64)

            def tokens_in(u, k, q):
                pe.wait_ge(s_g[k], u.count(4, 16 - 4 * k))
                if positive(n := u.count(1, -1)):
                    pe.wait_ge(s_gT, n)
                tr(bank[q][:, 0:P], xg[:, k, :], ident).then_inc(s_gt, 1)

            def expert(eng, i, k):
                return eng.value_load(etile_i[0:1, bass.ds(i * RING + k, 1)], min_val=0,
                                      max_val=E0 - 1)

            def hidden_t0(u, q):
                pe.wait_ge(s_h, u.count(1, 1))
                if positive(n := u.count(1, -1)):
                    pe.wait_ge(s_hT, n)
                for c in range(4):
                    last = tr(bank[4 + q][:, c * P:(c + 1) * P], h0[:, q, c * P:(c + 1) * P], ident)
                last.then_inc(s_htr, 1)

            def out0(u, q, e):
                pe.wait_ge(s_hT, u.count(1, 1))
                if positive(n := u.count(1, -1)):
                    pe.wait_ge(s_y, n)
                for c in range(4):
                    last = mm(bank[6 + q][:, 0:P], h0T[:, q, c * P:(c + 1) * P],
                              w2T0[:, bass.ds(e, 1), c, :].rearrange("p o d -> p (o d)"),
                              start=(c == 0), stop=(c == 3))
                last.then_inc(s_yps, 1)

            def tile0(i, k, first):
                u = Unit(0, i, RING, k)
                p = u.shift(-1)
                q = k % 2
                tokens_in(u, k, q)
                if not first or k > 0:
                    hidden_t0(p, 1 - q)
                e = expert(pe, i, k)
                pe.wait_ge(s_gT, u.count(1, 1))
                if positive(n := u.count(1, -1)):
                    pe.wait_ge(s_h, n)
                mm(bank[2 + q][:, :], xgT[:, q, :],
                   w1T0[:, bass.ds(e, 1), :].rearrange("p o f -> p (o f)"),
                   start=True, stop=True).then_inc(s_hps, 1)
                if not first or k > 0:
                    out0(p, 1 - q, expert(pe, i, k - 1))

            def end0(last):
                u = Unit(0, last, RING, RING - 1)
                hidden_t0(u, 1)
                out0(u, 1, expert(pe, last, RING - 1))

            ring_rounds(pe, TILES0, tile0, end0)

            pe.wait_ge(s_prep, 6)

            def project(h, b, w, x, T, done):
                for c in range(4):
                    last = mm(b[:, c * T:(c + 1) * T], w[:, c * P:(c + 1) * P], x,
                              start=True, stop=True)
                last.then_inc(done, 1)

            def half_b(at):
                u, t, t2, t3, t4, h, h2 = at(0), at(-1), at(-2), at(-3), at(-4), at(1), at(2)
                y = cT if h and h.a else zT
                scores_ahead(u, h, 0)
                if u:
                    transposes(u, 0)
                if h:
                    pe.wait_ge(s_zT, h.n(1, 1))
                    project(h, m0, wq[h.a], zT[:, :], TOK, s_qps)
                if t2:
                    if t3:
                        pe.wait_ge(s_sum, t3.l(1, 1))
                    pe.wait_ge(s_z3, t2.l(1, 1))
                    tr(m1[:, 0:P], z3[:, :], ident).then_inc(s_z3t, 1)
                if t:
                    if t4 and t4.a:
                        pe.wait_ge(s_lg, t4.gb(1, 1))
                    spread(t)
                    values(t, 3)
                if h:
                    pe.wait_ge(s_q, h.n(1, 1))
                    project(h, m0, wk[h.a][0:h.rk, :], y[:, :], h.T, s_kps)

                scores_ahead(u, h, 1)
                if u:
                    transposes(u, 1)
                if t2:
                    pe.wait_ge(s_z3T, t2.l(1, 1))
                    for c in range(4):
                        last = mm(m1[:, c * P:(c + 1) * P], li2[t2.a][:, c * P:(c + 1) * P],
                                  z3T[:, :], start=True, stop=True)
                    last.then_inc(s_li2, 1)
                if h:
                    pe.wait_ge(s_k, h.n(1, 1))
                    mm(m0[0:h.T, :], y[:, :], wv[h.a][0:h.rk, :], start=True, stop=True)\
                        .then_inc(s_vps, 1)
                if u:
                    values(u, 0)

                scores_ahead(u, h, 2)
                if u:
                    transposes(u, 2)
                if t:
                    if h:
                        pe.wait_ge(s_v, h.n(1, 1))
                    pe.wait_ge(s_oT, t.n(1, 1))
                    for g in range(4):
                        last = mm(m0[:, 0:P], oT[:, t.slot, g * P:(g + 1) * P],
                                  li1[t.a][:, g * P:(g + 1) * P], start=(g == 0), stop=(g == 3))
                    last.then_inc(s_li1, 1)
                if t and (t3 and t3.a or t4 and t4.a):
                    pe.wait_ge(s_rs, t.n(1, 1))
                if t3 and t3.a:
                    router_transpose(t3, dbank)
                if t4 and t4.a:
                    router_counts(t4, dbank, E1)
                if u:
                    values(u, 1)

                scores_ahead(u, h, 3)
                if u:
                    transposes(u, 3)
                if t2:
                    pe.wait_ge(s_gelu, t2.l(1, 1))
                    for c in range(4):
                        last = mm(m1[:, 0:P], hT[:, c * P:(c + 1) * P], li3[t2.a][:, c * P:(c + 1) * P],
                                  start=(c == 0), stop=(c == 3))
                    last.then_inc(s_li3, 1)
                if t3 and t3.a:
                    router_logits(t3, dbank, rw1, E1)
                if u:
                    values(u, 2)
                if h2:
                    if t:
                        pe.wait_ge(s_xo, t.l(1, 1))
                    elif h:
                        pe.wait_ge(s_v, h.n(1, 1))
                    inputs_T(h2)
                if t4 and t4.a:
                    pe.wait_ge(s_cumr, t4.gb(1, 1))

            pipeline_b(pe, half_b)

            pe.wait_ge(s_w1, 32)

            def glu_t(u, q):
                pe.wait_ge(s_h, u.count(1, 1))
                pe.wait_ge(s_hT, u.count(1, -1))
                pe.nop(nofuse=True)
                tr(bank[4 + q][:, 0:P], glu[:, q, :], ident).then_inc(s_htr, 1)

            def out1(u, q, i, k):
                pe.wait_ge(s_hT, u.count(1, 1))
                pe.wait_ge(s_y, u.count(1, -1))
                if positive(n := Unit(0, u.i, RING, u.r).count(1, -1)):
                    pe.wait_ge(s_yl, n)
                mm(bank[6 + q][:, 0:P], h0T[:, q, 0:P],
                   w2_1[:, bass.ds(i * (RING // 2) + k // 2, 1), :].rearrange("p o h -> p (o h)"),
                   start=True, stop=True).then_inc(s_yps, 1)

            def tile1(i, k, first):
                u = Unit(TILES0, i, RING, k)
                p = u.shift(-1)
                q = k % 2
                tokens_in(u, k, q)
                if not first or k > 0:
                    glu_t(p, 1 - q)
                pe.wait_ge(s_gT, u.count(1, 1))
                pe.wait_ge(s_h, u.count(1, -1))
                mm(bank[2 + q][:, 0:P], xgT[:, q, :],
                   w1_1[:, bass.ds(i * RING + k, 1), :].rearrange("p o f -> p (o f)"),
                   start=True, stop=True).then_inc(s_hps, 1)
                if not first or k > 0:
                    out1(p, 1 - q, i, k - 1)

            def end1(last):
                u = Unit(TILES0, last, RING, RING - 1)
                glu_t(u, 1)
                out1(u, 1, last, RING - 1)

            ring_rounds(pe, E1, tile1, end1)

            pe.wait_ge(s_y127d, 16)

            def step_c(i, k):
                u = Unit(0, i, RING, k)
                q = k % 2
                pe.wait_ge(s_po, u.count(1, 1))
                if positive(n := u.count(1, -1)):
                    pe.wait_ge(s_poT, n)
                    pe.nop(nofuse=True)
                tr(bank[q][0:E1, 0:P], poS[:, k, 0:E1], ident).then_inc(s_pot, 1)
                pe.wait_ge(s_poT, u.count(1, 1))
                if positive(n := u.count(1, -1)):
                    pe.wait_ge(s_acc, n)
                mm(bank[2 + q][:, 0:P], poT[0:E1, k, :], y127[:, :], start=True, stop=True)\
                    .then_inc(s_ov, 1)

            for k in range(RING):
                step_c(0, k)
            with pe.Fori(1, NB // RING) as i:
                for k in range(RING):
                    step_c(i, k)

        @block.scalar
        def _(act):
            af = nc.scalar.activation

            def exps(u, g):
                act.wait_ge(s_max, u.n(4, g + 1))
                if positive(n := u.n(4, g - 1)):
                    act.wait_ge(s_tr, n)
                T = u.T
                for c in range(4):
                    last = af(prob[:, g % 2, c * T:(c + 1) * T], sbank[g % 2][:, c * T:(c + 1) * T],
                              ACT.Exp, bias=nmax[:, g % 2, c:c + 1],
                              accum_out=den[:, u.slot, 4 * g + c:4 * g + c + 1])
                last.then_inc(s_exp, 1)

            def exps_ahead(u, h, g):
                if g < 2 and u:
                    exps(u, g + 2)
                if g >= 2 and h:
                    exps(h, g - 2)

            def pt_even(u, g):
                act.wait_ge(s_tr, u.n(4, g + 1))
                if positive(n := u.n(4, g - 1)):
                    act.wait_ge(s_pv, n)
                af(pT[0:u.T, 0, :], tbank[0][0:u.T, :], ACT.Copy).then_inc(s_pt[0], 1)

            def copy_spread(t, width):
                act.wait_ge(s_r, t.n(1, 1))
                if positive(n := t.n(1, 0)):
                    act.wait_ge(s_oT, n)
                af(rS[:, 0:width], dbank[:, 0:width], ACT.Copy).then_inc(s_rs, 1)

            def inputs_T(h):
                act.wait_ge(s_ht, h.n(1, 1))
                if h.base == 0 or h.a:
                    af(cT[:, :], m0[0:LAT, P:P + CTX], ACT.Copy)
                af(zT[:, :], m0[:, 0:P], ACT.Copy).then_inc(s_zT, 1)

            def copy_xnT(v, b):
                act.wait_ge(s_xnt, v.gb(1, 1))
                af(xnT[:, :], b[:, 0:P], ACT.Copy).then_inc(s_xnT, 1)

            act.wait_ge(s_x[0], 32)

            def half_a(at):
                u, t, t2, h, h2 = at(0), at(-1), at(-2), at(1), at(2)
                if u:
                    pt_even(u, 0)
                if t:
                    copy_spread(t, P)
                exps_ahead(u, h, 0)
                if h2:
                    if positive(n := h2.n(1, 0)):
                        act.wait_ge(s_ht, n)
                    act.nop(nofuse=True)
                    af(cS[:, :], ctx_sb[:, h2.batch, :], ACT.Copy).then_inc(s_c, 1)
                exps_ahead(u, h, 1)
                if t2:
                    copy_xnT(t2, dbank)
                if u:
                    pt_even(u, 2)
                exps_ahead(u, h, 2)
                exps_ahead(u, h, 3)
                if h2:
                    inputs_T(h2)

            pipeline_a(act, half_a, before_loop=lambda: act.wait_ge(s_x[1], 32))

            def relu(u, q):
                act.wait_ge(s_htr, u.count(1, 1))
                if positive(n := u.count(1, -1)):
                    act.wait_ge(s_yps, n)
                af(h0T[:, q, :], bank[4 + q][:, :], ACT.Relu).then_inc(s_hT, 1)

            ring_rounds(act, TILES0, lambda i, k, first: relu(Unit(0, i, RING, k), k % 2),
                        lambda last: None)

            def half_b(at):
                u, t, t2, t3, t4, h, h2 = at(0), at(-1), at(-2), at(-3), at(-4), at(1), at(2)
                if u:
                    pt_even(u, 0)
                if t2:
                    act.wait_ge(s_z3t, t2.l(1, 1))
                    af(z3T[:, :], m1[:, 0:P], ACT.Copy).then_inc(s_z3T, 1)
                if t:
                    copy_spread(t, 512)
                exps_ahead(u, h, 0)

                exps_ahead(u, h, 1)
                if t4 and t4.a:
                    act.wait_ge(s_v8, t4.b(1, 1))
                    af(expl[:, :], lg[:, :], ACT.Exp, bias=nv0[:, :], accum_out=esum[:, :])
                    af(e4[:, :], v8[:, 0:TOPK], ACT.Exp, bias=nv0[:, :]).then_inc(s_el, 1)
                if t2:
                    act.wait_ge(s_li2, t2.l(1, 1))
                    if positive(n := t2.l(1, 0)):
                        act.wait_ge(s_li3, n)
                    for c in range(4):
                        last = af(hT[:, c * P:(c + 1) * P], m1[:, c * P:(c + 1) * P], ACT.Gelu,
                                  bias=b2c[t2.a][:, c:c + 1])
                    last.then_inc(s_gelu, 1)

                if u:
                    pt_even(u, 2)
                exps_ahead(u, h, 2)
                if t3 and t3.a:
                    copy_xnT(t3, dbank)

                exps_ahead(u, h, 3)
                if t3 and t3.a:
                    act.wait_ge(s_lgps, t3.gb(1, 1))
                    if positive(n := t3.b(1, 0)):
                        act.wait_ge(s_dest, t3.gb(1, 0))
                    af(lg[:, :], dbank[:, 0:E1], ACT.Copy).then_inc(s_lg, 1)
                if h2:
                    inputs_T(h2)

            pipeline_b(act, half_b)

            def silu_part(u, q):
                act.wait_ge(s_hps, u.count(1, 1))
                act.wait_ge(s_h, u.count(1, -1))
                af(silu[:, q, 0:I1], bank[2 + q][:, 0:I1], ACT.Silu).then_inc(s_sil, 1)

            def last_slot(u, k, q):
                act.wait_ge(s_y, u.count(1, 1))
                af(ylast[96:128, k, :], bank[6 + q][96:128, 0:P], ACT.Copy).then_inc(s_yl, 1)

            def tile1(i, k, first):
                u = Unit(TILES0, i, RING, k)
                silu_part(u, k % 2)
                if positive(n := i * 16):
                    act.wait_ge(s_yld[k], n)
                if not first or k > 0:
                    last_slot(u.shift(-1), (k - 1) % RING, (k - 1) % 2)

            ring_rounds(act, E1, tile1,
                        lambda last: last_slot(Unit(TILES0, last, RING, RING - 1), RING - 1, 1))

            def step_c(i, k):
                u = Unit(0, i, RING, k)
                if positive(n := u.count(1, -3)):
                    act.wait_ge(s_pot, n)
                    act.nop(nofuse=True)
                af(poS[:, k, 0:E1], pover[:, bass.ds(i * RING + k, 1), :].rearrange("p o e -> p (o e)"),
                   ACT.Copy).then_inc(s_po, 1)
                act.wait_ge(s_pot, u.count(1, 1))
                if positive(n := u.count(1, -3)):
                    act.wait_ge(s_ov, n)
                af(poT[0:E1, k, :], bank[k % 2][0:E1, 0:P], ACT.Copy).then_inc(s_poT, 1)

            for k in range(RING):
                step_c(0, k)
            with act.Fori(1, NB // RING) as i:
                for k in range(RING):
                    step_c(i, k)

        @block.gpsimd
        def _(pool):
            g_ = nc.gpsimd

            def rstd(st, rows=P):
                return g_.tensor_tensor(st[0:rows, 9:10], st[0:rows, 8:9], neghalf[0:rows, :], ALU.pow)

            pool.wait_ge(s_const, 32)

            def half_a(at):
                t, t3, h2 = at(-1), at(-3), at(2)
                if h2:
                    pool.wait_ge(s_hvar, h2.n(1, 1))
                    pool.nop(nofuse=True)
                    rstd(st_h).then_inc(s_hrstd, 1)
                if t:
                    pool.wait_ge(s_nvar, t.n(1, 1))
                    pool.nop(nofuse=True)
                    rstd(st_n).then_inc(s_nrstd, 1)
                if t3:
                    if t3.off == 0 and isinstance(t3.i, int):
                        pool.wait_ge(s_init, 16 * NINIT)
                    pool.wait_ge(s_dest, t3.n(1, 1))
                    pool.nop(nofuse=True)
                    g_.indirect_dma_start(out=list0_d, out_offset=bass.IndirectOffsetOnAxis(
                        ap=dest[:, t3.bs, 0:1], axis=0), in_=tokid[:, t3.bs:t3.bs + 1],
                        in_offset=None).then_inc(s_sc[t3.bs], 16)

            pipeline_a(pool, half_a)

            def gather(u, k, src, ready):
                ready(u, k)
                if positive(n := u.count(1, -3)):
                    pool.wait_ge(s_gt, n)
                    pool.nop(nofuse=True)
                g_.indirect_dma_start(out=xg[:, k, :], out_offset=None, in_=src,
                                      in_offset=bass.IndirectOffsetOnAxis(
                                          ap=ids[:, k:k + 1].bitcast(U32), axis=0))\
                    .then_inc(s_g[k], 16)

            def scatter(u, k, dst, idx):
                pool.wait_ge(s_y, u.count(1, 1))
                pool.nop(nofuse=True)
                g_.indirect_dma_start(out=dst, out_offset=bass.IndirectOffsetOnAxis(
                    ap=idx[:, k:k + 1].bitcast(U32), axis=0), in_=yS[:, k, :], in_offset=None,
                    bounds_check=dst.shape[0] - 1, oob_is_err=False)\
                    .then_inc(s_ysc[k], 16)

            def experts(n, base, src, dst, idx, ready):
                LAG = 2

                def step(i, k, first):
                    u = Unit(base, i, RING, k)
                    gather(u, k, src, ready)
                    if not first or k >= LAG:
                        scatter(u.shift(-LAG), (k - LAG) % RING, dst, idx)

                def after(last):
                    for k in range(RING - LAG, RING):
                        scatter(Unit(base, last, RING, k), k, dst, idx)

                ring_rounds(pool, n, step, after)

            for s in range(2):
                pool.wait_ge(s_xnd[s], 16 * (NB // 2))
            experts(TILES0, 0, xn0_d, y0_d, ids,
                    lambda u, k: pool.wait_ge(s_ids[k], u.i * 16 + 16))

            def mask_chunk(u, g):
                pool.wait_ge(s_pt[g % 2], u.n(2, g // 2 + 1))
                pool.nop(nofuse=True)
                pool.wait_ge(s_pv, u.n(4, g - 1))
                pool.nop(nofuse=True)
                g_.affine_select(out=pTm[:, g % 2, :], in_=pT[:, g % 2, :], compare_op=ALU.is_gt,
                                 fill=0.0, base=0, pattern=[[0, 4], [-1, P]],
                                 channel_multiplier=1).then_inc(s_ptm, 1)

            def half_b(at):
                u, t, t2, t3, t5, h2 = at(0), at(-1), at(-2), at(-3), at(-5), at(2)
                masked = u and u.a == 0
                if masked:
                    mask_chunk(u, 0)
                if h2:
                    pool.wait_ge(s_hvar, h2.n(1, 1))
                    pool.nop(nofuse=True)
                    rstd(st_h).then_inc(s_hrstd, 1)
                    if h2.a:
                        pool.wait_ge(s_cvar, h2.b(1, 1))
                        pool.nop(nofuse=True)
                        rstd(st_c, CTX).then_inc(s_crstd, 1)
                if masked:
                    mask_chunk(u, 1)
                if t3 and t3.a:
                    pool.wait_ge(s_nvar, t3.gb(1, 1))
                    pool.nop(nofuse=True)
                    rstd(st_n).then_inc(s_nrstd, 1)
                if t2:
                    g_.tensor_tensor(ssa[:, :], xxb[:, t2.ring, :], xo[:, :], ALU.add)
                    pool.drain()
                    if t2.a:
                        g_.tensor_tensor(ssb[:, :], ssa[:, :], xres[:, t2.batch, :], ALU.add)
                        pool.drain()
                    if positive(n := t2.l(1, 0)):
                        pool.wait_ge(s_sum, n)
                        pool.nop(nofuse=True)
                    g_.tensor_tensor(ss[:, :], (ssb if t2.a else ssa)[:, :], li3b[t2.a][:, :], ALU.add)\
                        .then_inc(s_ss, 1)
                if h2:
                    pool.wait_ge(s_xvar, h2.l(1, 1))
                    pool.nop(nofuse=True)
                    rstd(st_x).then_inc(s_xrstd, 1)
                    if positive(n := h2.l(1, -3)):
                        pool.wait_ge(s_xo, n)
                        pool.nop(nofuse=True)
                    g_.tensor_tensor(xxb[:, h2.ring, :], xx[:, :], li1b[h2.a][:, :], ALU.add)\
                        .then_inc(s_xxb, 1)
                if masked:
                    mask_chunk(u, 2)
                    mask_chunk(u, 3)
                if t:
                    pool.wait_ge(s_3var, t.l(1, 1))
                    pool.nop(nofuse=True)
                    rstd(st_3).then_inc(s_3rstd, 1)
                if t5 and t5.a:
                    pool.wait_ge(s_dest, t5.gb(1, 1))
                    pool.nop(nofuse=True)
                    for k in range(TOPK):
                        g_.indirect_dma_start(out=list1_d, out_offset=bass.IndirectOffsetOnAxis(
                            ap=dest[:, t5.bs, k:k + 1], axis=0), in_=pay[:, t5.bs, k, :],
                            in_offset=None, bounds_check=SLOTS1 - 1, oob_is_err=False)\
                            .then_inc(s_sc1[t5.bs], 16)

            pipeline_b(pool, half_b)

            for s in range(2):
                pool.wait_ge(s_xnd[s], 16 * NB)
            pool.wait_ge(s_c0, 16 * (CROWS // (4 * P)))
            def indices_there(u, k):
                pool.wait_ge(s_idx, Unit(0, u.i, RING, u.r).count(1, 1))
                pool.nop(nofuse=True)

            experts(E1, TILES0, xn1_d, c_d, idr, indices_there)

            def step_c(i, k):
                u = Unit(0, i, RING, k)
                pool.wait_ge(s_cld[k], u.i * 16 + 16)
                pool.nop(nofuse=True)
                if positive(n := u.count(1, -1)):
                    pool.wait_ge(s_fin, n)
                    pool.nop(nofuse=True)
                g_.tensor_tensor(csum2[:, k % 2, 0:256], cb[k][:, 0:256], cb[k][:, 256:512],
                                 ALU.add).then_inc(s_cs, 1)

            for k in range(RING):
                step_c(0, k)
            with pool.Fori(1, NB // RING) as i:
                for k in range(RING):
                    step_c(i, k)

        @block.vector
        def _(dve):
            v_ = nc.vector

            def after():
                dve.drain()

            def copy(o, i):
                return v_.tensor_copy(o, i)

            def norm_stats(st, src, done, rows=P, a=1.0, c=EPS):
                v_.bn_stats(st[0:rows, 0:6], src)
                after()
                v_.bn_aggr(st[0:rows, 6:8], st[0:rows, 0:6])
                after()
                v_.tensor_scalar(st[0:rows, 8:9], st[0:rows, 7:8], a, c, ALU.mult, ALU.add)\
                    .then_inc(done, 1)

            def normalise(dst, src, st, rows=P):
                return v_.tensor_scalar(dst, src, st[0:rows, 6:7], st[0:rows, 9:10],
                                        ALU.subtract, ALU.mult)

            def maxima(u, g):
                T = u.T
                dve.wait_ge(s_s, u.n(4, g + 1))
                if positive(n := u.n(4, g - 1)):
                    dve.wait_ge(s_exp, n)
                v_.tensor_reduce(nmax[:, g % 2, :],
                                 sbank[g % 2][:, 0:4 * T].rearrange("p (j t) -> p j t", j=4),
                                 AX.X, ALU.max, negate=True).then_inc(s_max, 1)

            def maxima_ahead(u, h, g):
                if g < 2 and u:
                    maxima(u, g + 2)
                if g >= 2 and h:
                    maxima(h, g - 2)

            def pt_odd(u, g):
                dve.wait_ge(s_tr, u.n(4, g + 1))
                if positive(n := u.n(4, g - 1)):
                    dve.wait_ge(s_pv, n)
                copy(pT[0:u.T, 1, :], tbank[1][0:u.T, :]).then_inc(s_pt[1], 1)

            def denominators(u):
                dve.wait_ge(s_exp, u.n(4, 4))
                v_.reciprocal(rd[:, :], den[:, u.slot, :])
                after()
                if positive(n := u.n(1, 0)):
                    dve.wait_ge(s_r, n)
                if u.base == 0:
                    last = copy(rdx[:, 0:P].rearrange("p (j g x) -> p j g x", j=4, x=D0),
                                rd[:, :].rearrange("p (g j) -> p j g", j=4).unsqueeze(3)
                                .to_broadcast([P, 4, 4, D0]))
                else:
                    last = copy(rdx[:, :].rearrange("p (h x) -> p h x", x=D1),
                                rd[:, :].unsqueeze(2).to_broadcast([P, HEADS, D1]))
                last.then_inc(s_rd, 1)

            def finish_core(u, width):
                dve.wait_ge(s_rs, u.n(1, 1))
                dve.wait_ge(s_pv, u.n(4, 4))
                v_.tensor_tensor(oT[:, u.slot, 0:width], obank[:, 0:width], rS[:, 0:width],
                                 ALU.mult).then_inc(s_oT, 1)

            def bcast(col, n):
                return col.unsqueeze(2).to_broadcast([P, 4, n])

            v_.memset(zeros[:, :], 0.0).then_inc(s_made, 1)
            v_.memset(onesb[:, :], 1.0)
            v_.memset(count0[:, :], 0.0)
            v_.memset(count1[:, :], 0.0)
            v_.memset(vS[:, :, :], 0.0)
            v_.memset(kbd[:, :, :], 0.0).then_inc(s_made, 1)
            dve.wait_ge(s_const, 32)
            copy(ltri[:, :], ltri_f).then_inc(s_made, 1)
            for s in range(2):
                copy(pay_i[:, s, :, 0], cst_i[:, 258 + 4 * s:262 + 4 * s])
            dve.wait_ge(s_load, 16 * N_LOADS)
            v_.tensor_scalar(wqT0[:, :], wqT0[:, :], float(D0) ** -0.5, None, ALU.mult)\
                .then_inc(s_made, 1)
            dve.wait_ge(s_x[0], 32)

            def project_a(h):
                s = h.slot
                dve.wait_ge(s_qps, h.n(1, 1))
                copy(qT[:, s, 0:P], m1[:, 0:P]).then_inc(s_q, 1)
                if positive(n := h.n(16, 0)):
                    dve.wait_ge(s_kd[3], n)
                v_.tensor_tensor(kT[:, 0:4 * CTX].rearrange("p (j t) -> p j t", j=4),
                                 m1[:, P:P + CTX].unsqueeze(1).to_broadcast([P, 4, CTX]),
                                 bcast(kmask, CTX), ALU.mult).then_inc(s_k, 1)
                if positive(n := h.n(4, -4)):
                    dve.wait_ge(s_pv, n)
                for g in range(4):
                    last = copy(vS[0:CTX, s, g * P:(g + 1) * P]
                                .rearrange("p (j c) -> p j c", j=4)[:, :, 8 * g:8 * g + 8],
                                m1[0:CTX, 256 + 32 * g:288 + 32 * g].rearrange("p (j d) -> p j d", j=4))
                last.then_inc(s_v, 1)

            def choose_a(v):
                dve.wait_ge(s_lg, v.n(1, 1))
                dve.nop(nofuse=True)
                v_.max(out=v8[:, :], in_=lg[:, 0:E0])
                after()
                v_.max_index(i8[:, :], v8[:, :], lg[:, 0:E0])
                after()
                copy(i8f[:, 0:1], i8[:, 0:1])
                after()
                v_.tensor_scalar(mask_f[:, 0:E0], iota64[:, 0:E0], i8f[:, 0:1], None, ALU.is_equal)
                v_.tensor_scalar(mask_b[:, 0:E0], iota64[:, 0:E0], i8f[:, 0:1], None, ALU.is_equal)\
                    .then_inc(s_mask, 1)

            def dest_a(v):
                s = v.bs
                dve.wait_ge(s_cum, v.n(1, 1))
                v_.tensor_tensor(pos[:, 0:E0], m1[:, 0:E0], count0[:, :], ALU.add)
                after()
                v_.tensor_tensor(count0[:, :], m1[:, E0:2 * E0], count0[:, :], ALU.add)\
                    .then_inc(s_cumr, 1)
                v_.tensor_tensor(posw[:, 0:E0], pos[:, 0:E0], slot0, ALU.add)
                after()
                v_.tensor_tensor(pos[:, 0:E0], posw[:, 0:E0], mask_f[:, 0:E0], ALU.mult)
                after()
                v_.tensor_reduce(dest_f[:, 0:1], pos[:, 0:E0], AX.X, ALU.add)
                after()
                if positive(n := v.pair(16)):
                    dve.wait_ge(s_sc[s], n)
                v_.tensor_scalar(tokid[:, s:s + 1], tokid[:, s:s + 1], 2.0 * P, None, ALU.add)
                copy(dest[:, s, 0:1], dest_f[:, 0:1]).then_inc(s_dest, 1)

            def half_a(at):
                u, t, t2, t3, h, h2 = at(0), at(-1), at(-2), at(-3), at(1), at(2)
                maxima_ahead(u, h, 0)
                if h:
                    project_a(h)
                if h2:
                    norm_stats(st_h, xres[:, h2.batch, :], s_hvar)
                if t:
                    finish_core(t, P)
                if t2:
                    dve.wait_ge(s_nrstd, t2.n(1, 1))
                    if positive(n := t2.pair(16)):
                        dve.wait_ge(s_xnd[t2.bs], n)
                    normalise(xnS[:, t2.bs, :], xres[:, t2.batch, :], st_n).then_inc(s_xn, 1)

                maxima_ahead(u, h, 1)
                if u:
                    pt_odd(u, 1)
                if t3:
                    choose_a(t3)
                if h2:
                    dve.wait_ge(s_hrstd, h2.n(1, 1))
                    normalise(zS[:, :], xres[:, h2.batch, :], st_h).then_inc(s_z, 1)

                maxima_ahead(u, h, 2)
                if t:
                    dve.wait_ge(s_li1, t.n(1, 1))
                    v_.tensor_tensor(xres[:, t.batch, :], xres[:, t.batch, :], m0[:, 0:P], ALU.add)
                    after()
                    norm_stats(st_n, xres[:, t.batch, :], s_nvar)

                maxima_ahead(u, h, 3)
                if t3:
                    dest_a(t3)
                if u:
                    denominators(u)
                    pt_odd(u, 3)
                if t2:
                    dve.wait_ge(s_lgps, t2.n(1, 1))
                    v_.tensor_tensor(lg[:, 0:E0], dbank[:, 0:E0], br0[:, :], ALU.add).then_inc(s_lg, 1)

            pipeline_a(dve, half_a, before_loop=lambda: dve.wait_ge(s_x[1], 32))

            after()
            v_.tensor_scalar(nt_i[:, :], count0[0:1, :], float(P - 1), None, ALU.add)
            after()
            v_.tensor_scalar(nt_i[:, :], nt_i[:, :], 7, None, ALU.logical_shift_right)
            after()
            copy(nt_f[:, :], nt_i[:, :])
            after()
            v_.tensor_tensor_scan(ends[:, :], ones32[0:1, 0:E0], nt_f[:, :], 0.0, ALU.mult, ALU.add)
            after()
            jb = tilenum.unsqueeze(2).to_broadcast([1, TILES0, 7])
            v_.tensor_tensor(mp, jb, ends[:, 0:7].unsqueeze(1).to_broadcast([1, TILES0, 7]), ALU.is_ge)
            after()
            v_.tensor_reduce(etile[:, :], mp, AX.X, ALU.add)
            v_.tensor_tensor(mp2, mp, nt_f[:, 0:7].unsqueeze(1).to_broadcast([1, TILES0, 7]), ALU.mult)
            after()
            v_.tensor_reduce(stile[:, :], mp2, AX.X, ALU.add)
            after()
            v_.tensor_tensor(btile[:, :], tilenum, stile[:, :], ALU.subtract)
            after()
            v_.tensor_scalar(stile[:, :], etile[:, :], float(NTOK), None, ALU.mult)
            after()
            v_.scalar_tensor_tensor(base_i[:, :], btile[:, :], float(P), stile[:, :], ALU.mult, ALU.add)
            copy(etile_i[:, :], etile[:, :]).then_inc(s_map, 1)

            SCALE = float(D1) ** -0.5
            for a in range(2):
                rk = LAT if a else P
                if a:
                    after()
                copy(tmp[0:rk, :], cols[0:rk, a, 3:4].to_broadcast([rk, P])).then_inc(s_prep, 1)
                dve.wait_ge(s_prep_pe, a + 1)
                v_.tensor_scalar(bq[a][:, :], m0[:, 0:4], SCALE, None, ALU.mult)
                copy(bk[a][:, :], m0[:, 4:8])
                v_.tensor_tensor(b2c[a][:, :], m0[:, 8:12], b2c[a][:, :], ALU.add)
                copy(bv[a][:, :], m1[:, :]).then_inc(s_prep, 1)
                v_.tensor_scalar(wq[a][:, :], wq[a][:, :], cols[:, a, 0:1], SCALE, ALU.mult, ALU.mult)
                v_.tensor_scalar(wk[a][0:rk, :], wk[a][0:rk, :], cols[0:rk, a, 2:3], None, ALU.mult)
                v_.tensor_scalar(wv[a][0:rk, :], wv[a][0:rk, :], cols[0:rk, a, 2:3], None, ALU.mult)
                v_.tensor_tensor(li3b[a][:, :], li3b[a][:, :], li1b[a][:, :], ALU.subtract)
                v_.tensor_scalar(li2[a][:, :], li2[a][:, :], cols[:, a, 4:5], None, ALU.mult)\
                    .then_inc(s_prep, 1)

            dve.wait_ge(s_ffnw, 64)

            def expert(i, k):
                return dve.value_load(etile_i[0:1, bass.ds(i * RING + k, 1)], min_val=0,
                                      max_val=E0 - 1)

            def tokens_T(u, k, q):
                dve.wait_ge(s_gt, u.count(1, 1))
                if positive(n := u.count(1, -1)):
                    dve.wait_ge(s_hps, n)
                copy(xgT[:, q, :], bank[q][:, 0:P]).then_inc(s_gT, 1)

            def hidden0(u, q, e):
                dve.wait_ge(s_hps, u.count(1, 1))
                if positive(n := u.count(1, -1)):
                    dve.wait_ge(s_htr, n)
                v_.tensor_tensor(h0[:, q, :], bank[2 + q][:, :],
                                 b1bc0[:, bass.ds(e, 1), :].rearrange("p o f -> p (o f)"), ALU.add)\
                    .then_inc(s_h, 1)

            def result0(u, k, e):
                dve.wait_ge(s_yps, u.count(1, 1))
                v_.tensor_tensor(yS[:, k, :], bank[6 + k % 2][:, 0:P],
                                 b2bc0[:, bass.ds(e, 1), :].rearrange("p o d -> p (o d)"), ALU.add)\
                    .then_inc(s_y, 1)

            def tile0(i, k, first):
                u = Unit(0, i, RING, k)
                if positive(n := i * 16):
                    dve.wait_ge(s_ysc[k], n)
                tokens_T(u, k, k % 2)
                hidden0(u, k % 2, expert(i, k))
                if not first or k > 0:
                    result0(u.shift(-1), (k - 1) % RING, expert(i, k - 1))

            ring_rounds(dve, TILES0, tile0,
                        lambda last: result0(Unit(0, last, RING, RING - 1), RING - 1,
                                             expert(last, RING - 1)))

            def context_norm(h, step):
                if step == 0:
                    norm_stats(st_c, ctx_sb[:, h.batch, :], s_cvar, CTX)
                else:
                    dve.wait_ge(s_crstd, h.b(1, 1))
                    if positive(n := h.n(1, 0)):
                        dve.wait_ge(s_ht, n)
                    dve.nop(nofuse=True)
                    normalise(cS[:, :], ctx_sb[:, h.batch, :], st_c, CTX).then_inc(s_c, 1)

            def first_norm(h):
                if h.a == 0:
                    s, b = h.bs, h.batch
                    dve.wait_ge(s_y0[s], h.pair(16) + 16)
                    v_.tensor_tensor(xres[:, b, :], xres[:, b, :], yb[:, s, :], ALU.add)\
                        .then_inc(s_x2, 1)
                    after()
                    norm_stats(st_h, xres[:, b, :], s_hvar, a=1.0 + EPS, c=EPS * EPS)
                else:
                    norm_stats(st_h, xp[:, h.bs, :], s_hvar)

            def second_norm(h):
                src = xp[:, h.bs, :] if h.a else xres[:, h.batch, :]
                dve.wait_ge(s_hrstd, h.n(1, 1))
                v_.scalar_tensor_tensor(tmp[:, :], src, st_h[:, 6:7], g_ln[h.a][:, :],
                                        ALU.subtract, ALU.mult)
                after()
                if positive(n := h.l(1, 0)):
                    dve.wait_ge(s_xxb, n)
                v_.scalar_tensor_tensor(xx[:, :], tmp[:, :], st_h[:, 9:10], b_ln[h.a][:, :],
                                        ALU.mult, ALU.add)
                after()
                norm_stats(st_x, xx[:, :], s_xvar)

            def queries(h):
                dve.wait_ge(s_qps, h.n(1, 1))
                v_.tensor_tensor(qT[:, h.slot, :].rearrange("p (c t) -> p c t", c=4),
                                 m0[:, :].rearrange("p (c t) -> p c t", c=4),
                                 bcast(bq[h.a][:, :], TOK), ALU.add).then_inc(s_q, 1)

            def keys(h):
                T = h.T
                dve.wait_ge(s_kps, h.l(1, 1))
                dve.wait_ge(s_kd[3], h.n(16, 0))
                v_.tensor_tensor(kT[:, 0:4 * T].rearrange("p (c t) -> p c t", c=4),
                                 m0[:, 0:4 * T].rearrange("p (c t) -> p c t", c=4),
                                 bcast(bk[h.a][:, :], T), ALU.add).then_inc(s_k, 1)

            def values(h):
                T = h.T
                dve.wait_ge(s_vps, h.l(1, 1))
                dve.wait_ge(s_pv, h.n(4, -4))
                v_.tensor_tensor(vS[0:T, h.slot, :], m0[0:T, :], bv[h.a][0:T, :], ALU.add)\
                    .then_inc(s_v, 1)

            def choose(v):
                dve.wait_ge(s_lg, v.gb(1, 1))
                dve.nop(nofuse=True)
                v_.max(out=v8[:, :], in_=lg[:, :])
                after()
                v_.tensor_scalar(nv0[:, :], v8[:, 0:1], -1.0, None, ALU.mult).then_inc(s_v8, 1)
                v_.max_index(i8[:, :], v8[:, :], lg[:, :])
                after()
                copy(i8f[:, :], i8[:, 0:TOPK])
                after()
                v_.tensor_tensor(oh4[:, :, :], iota64.unsqueeze(1).to_broadcast([P, TOPK, E1]),
                                 i8f[:, :].unsqueeze(2).to_broadcast([P, TOPK, E1]), ALU.is_equal)
                after()
                v_.tensor_reduce(mask_f[:, :], oh4[:, :, :].rearrange("p k e -> p e k"), AX.X, ALU.add)
                after()
                copy(mask_b[:, :], mask_f[:, :]).then_inc(s_mask, 1)

            def positions(v):
                if positive(n := v.pair(64)):
                    dve.wait_ge(s_sc1[v.bs], n)
                dve.wait_ge(s_cum, v.gb(1, 1))
                v_.tensor_tensor(pos[:, :], dbank[:, 0:E1], count1[:, :], ALU.add)
                after()
                v_.tensor_tensor(count1[:, :], dbank[:, E1:2 * E1], count1[:, :], ALU.add)\
                    .then_inc(s_cumr, 1)
                v_.scalar_tensor_tensor(posw[:, :], pos[:, :], float(E1), iota64, ALU.mult, ALU.add)
                v_.scalar_tensor_tensor(over[:, :], pos[:, :], float(CAP), mask_f[:, :],
                                        ALU.is_ge, ALU.mult).then_inc(s_pos, 1)

            def destinations(v):
                s = v.bs
                dve.wait_ge(s_pos, v.b(1, 1))
                dve.wait_ge(s_el, v.b(1, 1))
                v_.reciprocal(rsum[:, :], esum[:, :])
                v_.tensor_tensor(oh4s[:, :, :], oh4[:, :, :],
                                 posw[:, :].unsqueeze(1).to_broadcast([P, TOPK, E1]), ALU.mult)
                after()
                v_.scalar_tensor_tensor(pover[:, v.batch, :], expl[:, :], rsum[:, :], over[:, :],
                                        ALU.mult, ALU.mult)
                v_.tensor_reduce(dest_f[:, :], oh4s[:, :, :], AX.X, ALU.add)
                v_.tensor_scalar(pay_i[:, s, :, 0], pay_i[:, s, :, 0], 2.0 * P, None, ALU.add)
                v_.tensor_scalar(pay[:, s, :, 1], e4[:, :], rsum[:, :], None, ALU.mult)
                after()
                copy(dest[:, s, :], dest_f[:, :]).then_inc(s_dest, 1)

            def half_b(at):
                u, t, t2, t3, t4, t5 = at(0), at(-1), at(-2), at(-3), at(-4), at(-5)
                h, h2 = at(1), at(2)
                maxima_ahead(u, h, 0)
                if t2:
                    dve.wait_ge(s_3rstd, t2.l(1, 1))
                    normalise(z3[:, :], xo[:, :], st_3).then_inc(s_z3, 1)
                if h:
                    queries(h)
                if h2:
                    if h2.a:
                        dve.wait_ge(s_sum, t3.l(1, 1))
                        dve.nop(nofuse=True)
                    first_norm(h2)
                    if h2.a:
                        context_norm(h2, 0)
                if t:
                    finish_core(t, 512)
                if t3 and t3.a:
                    dve.wait_ge(s_sum, t3.l(1, 1))
                    dve.nop(nofuse=True)
                    norm_stats(st_n, xres[:, t3.batch, :], s_nvar)

                if h:
                    keys(h)
                maxima_ahead(u, h, 1)
                if t4 and t4.a:
                    choose(t4)
                if u:
                    pt_odd(u, 1)
                if h2:
                    second_norm(h2)
                if h:
                    values(h)
                if t3 and t3.a:
                    dve.wait_ge(s_nrstd, t3.gb(1, 1))
                    dve.wait_ge(s_xnd[t3.bs], t3.pair(16) + 16 * (NB // 2))
                    normalise(xnS[:, t3.bs, :], xres[:, t3.batch, :], st_n).then_inc(s_xn, 1)
                if t5 and t5.a:
                    destinations(t5)

                maxima_ahead(u, h, 2)
                if h2:
                    dve.wait_ge(s_xrstd, h2.l(1, 1))
                    dve.wait_ge(s_ht, h2.n(1, 0))
                    normalise(zS[:, :], xx[:, :], st_x).then_inc(s_z, 1)
                    if h2.a:
                        context_norm(h2, 1)
                if t:
                    dve.wait_ge(s_li1, t.n(1, 1))
                    dve.wait_ge(s_xxb, t.l(1, 1))
                    if positive(n := t.l(1, 0)):
                        dve.wait_ge(s_ss, n)
                    v_.tensor_tensor(xo[:, :], m0[:, 0:P], xxb[:, t.ring, :], ALU.add)\
                        .then_inc(s_xo, 1)
                    after()
                    norm_stats(st_3, xo[:, :], s_3var)

                maxima_ahead(u, h, 3)
                if u:
                    denominators(u)
                    pt_odd(u, 3)
                if t4 and t4.a:
                    positions(t4)
                if t2:
                    dve.wait_ge(s_ss, t2.l(1, 1))
                    dve.wait_ge(s_li3, t2.l(1, 1))
                    dst = xres[:, t2.batch, :] if t2.a else xp[:, t2.bs, :]
                    v_.tensor_tensor(dst, m1[:, 0:P], ss[:, :], ALU.add).then_inc(s_sum, 1)

            pipeline_b(dve, half_b)

            dve.wait_ge(s_l1, 16)
            v_.memset(list1[:, E1:E1 + 2, :], 0.0)
            after()

            def indices(i, k):
                k, i = k % RING, i + k // RING
                one = bass.ds(i * RING + k, 1)
                copy(wcol[:, k:k + 1], list1[:, one, 1])
                v_.tensor_scalar(ids[:, k:k + 1], list1_i[:, one, 0], NTOK - 1, None,
                                 ALU.bitwise_and).then_inc(s_idx, 1)

            def gate(u, q):
                dve.wait_ge(s_sil, Unit(0, u.i, RING, u.r).count(1, 1))
                dve.wait_ge(s_htr, u.count(1, -1))
                v_.tensor_tensor(glu[:, q, q * I1:(q + 1) * I1], bank[2 + q][:, I1:2 * I1], silu[:, q, 0:I1],
                                 ALU.mult).then_inc(s_h, 1)

            def gate_T(u, q):
                dve.wait_ge(s_htr, u.count(1, 1))
                dve.wait_ge(s_yps, u.count(1, -1))
                copy(h0T[:, q, 0:P], bank[4 + q][:, 0:P]).then_inc(s_hT, 1)

            def result1(u, k):
                dve.wait_ge(s_yps, u.count(1, 1))
                dve.wait_ge(s_ysc[k], Unit(u.base, u.i, RING, u.r - k).count(4))
                dve.nop(nofuse=True)
                copy(idr[:, k:k + 1], list1_i[:, bass.ds(u.i * RING + u.r, 1), 0])
                v_.tensor_scalar(yS[:, k, :], bank[6 + k % 2][:, 0:P], wcol[:, k:k + 1], None,
                                 ALU.mult).then_inc(s_y, 1)

            def tile1(i, k, first):
                u = Unit(TILES0, i, RING, k)
                p = u.shift(-1)
                tokens_T(u, k, k % 2)
                if not first or k > 0:
                    gate_T(p, (k - 1) % 2)
                gate(u, k % 2)
                if not first or k > 0:
                    result1(p, (k - 1) % RING)
                indices(i, k + 2)

            def end1(last):
                u = Unit(TILES0, last, RING, RING - 1)
                gate_T(u, 1)
                result1(u, RING - 1)

            for q in range(2):
                v_.memset(glu[:, q, (1 - q) * I1:(2 - q) * I1], 0.0)
            for k in range(2):
                indices(0, k)
            ring_rounds(dve, E1, tile1, end1)

            def step_c(i, k):
                u = Unit(0, i, RING, k)
                q = k % 2
                dve.wait_ge(s_ov, u.count(1, 1))
                v_.tensor_tensor(acc[:, k, :],
                                 xres[:, bass.ds(i * RING + k, 1), :].rearrange("p o d -> p (o d)"),
                                 bank[2 + q][:, 0:P], ALU.add).then_inc(s_acc, 1)
                dve.wait_ge(s_cs, u.count(1, 1))
                v_.tensor_tensor(acc2[:, k, :], csum2[:, q, 0:P], csum2[:, q, P:2 * P], ALU.add)
                after()
                if positive(n := i * 16):
                    dve.wait_ge(s_out[k], n)
                v_.tensor_tensor(outS[:, k, :], acc[:, k, :], acc2[:, k, :], ALU.add)\
                    .then_inc(s_fin, 1)

            for k in range(RING):
                step_c(0, k)
            with dve.Fori(1, NB // RING) as i:
                for k in range(RING):
                    step_c(i, k)


CST_WIDTH = 494 + 80
CSTI_WIDTH = 256 + 2 + 8


def constants(np, NB):
    ntok = NB * TOK
    c = np.zeros((P, CST_WIDTH), np.float32)
    p = np.arange(P)
    c[:, 0:128] = np.eye(P)
    c[:, 128:256] = p[:, None] < p[None, :]
    for g in range(NG):
        c[:, 256 + 32 * g + 8 * g:256 + 32 * g + 8 * g + 8] = 1.0
    c[:, 384:416] = 1.0
    c[:, 416:480] = np.arange(E1)
    c[:, 480:488] = np.arange(E0) * ntok
    c[:, 488:492] = (p[:, None] // D0) % 4 == np.arange(4)
    c[:, 493] = -0.5
    c[:, 494:574] = np.arange(80)
    n = np.zeros((P, CSTI_WIDTH), np.int32)
    n[:, 0:128] = ntok + np.arange(P)
    n[:, 128:256:2] = (TOPK * ntok + p)[:, None]
    for s in range(2):
        n[:, 256 + s] = p + TOK * s - 2 * TOK
        for k in range(TOPK):
            n[:, 258 + 4 * s + k] = k * ntok + p + TOK * s - 2 * TOK
    return c, n


def layouts(np, a):
    c = np.ascontiguousarray
    o = {"x": a["x"], "ctx": a["ctx_512"]}
    NB = a["x"].shape[0]
    o["cst"], o["cst_i"] = constants(np, NB)
    o["wqT0"] = c(a["L0_xattn_Wq"].T)
    o["wkvT0"] = c(a["L0_xattn_Wkv"].T)
    o["woT0"] = c(a["L0_xattn_Wo"].T.reshape(4, 4, D0, P).transpose(1, 0, 2, 3).reshape(P, P))
    o["wrT0"] = c(a["L0_ffn_Wr"].T)
    o["br0"] = a["L0_ffn_br"]
    o["w1T0"] = c(a["L0_ffn_W1"].transpose(2, 0, 1))
    o["w2T0"] = c(a["L0_ffn_W2"].reshape(E0, P, 4, P).transpose(3, 0, 2, 1))
    o["b10"] = a["L0_ffn_b1"]
    o["b20"] = a["L0_ffn_b2"]
    for k in range(2):
        m = f"L1_xattn_a{k + 1}_"
        for n in ("wq", "wk", "wv"):
            w = a[m + n]
            o[f"{n}{k}"] = c(w.transpose(1, 0, 2).reshape(w.shape[1], -1))
        o[f"li1{k}"] = c(a[m + "li1_w"].reshape(4, 4, D1, P).transpose(0, 2, 1, 3).reshape(P, 4 * P))
        o[f"li2{k}"] = a[m + "li2_w"]
        o[f"li3{k}"] = c(a[m + "li3_w"].reshape(4, P, P).transpose(1, 0, 2).reshape(P, 4 * P))
        o[f"b2c{k}"] = c(a[m + "li2_b"].reshape(4, P).T)
        o[f"li1b{k}"] = a[m + "li1_b"]
        o[f"li3b{k}"] = a[m + "li3_b"]
        o[f"g_ln{k}"] = a[f"L1_xattn_ln{k + 1}_g"]
        o[f"b_ln{k}"] = a[f"L1_xattn_ln{k + 1}_b"]
        for n in ("lnx", "lny", "ln3"):
            for x in "gb":
                o[f"{n}{x}{k}"] = a[f"{m}{n}_{x}"].reshape(-1, 1)
    o["router"] = a["L1_ffn_router_w"]
    o["w1_1"] = c(a["L1_ffn_w1"].transpose(1, 0, 2))
    o["w2_1"] = c(a["L1_ffn_w2"].reshape(E1 // 2, 2 * I1, P).transpose(1, 0, 2))
    return o


def kernel(**inputs):
    import numpy as np
    import concourse.bacc as bacc
    from concourse.bass_utils import run_bass_kernel_spmd

    a = {k: np.asarray(v) for k, v in inputs.items()}
    arrays = {f"in_{k}": np.ascontiguousarray(v) for k, v in layouts(np, a).items()}
    NB = a["x"].shape[0]
    nc = bacc.Bacc("TRN2", target_bir_lowering=False, num_devices=1)
    t = {k[3:]: nc.dram_tensor(k, v.shape, mybir.dt.from_np(v.dtype), kind="ExternalInput").ap()
         for k, v in arrays.items()}
    out = nc.dram_tensor("out", (NB * TOK, P), F32, kind="ExternalOutput").ap()
    build_program(nc, t, out, NB)
    r = run_bass_kernel_spmd(nc, [arrays], core_ids=[0])
    return r.results[0]["out"].reshape(NB, TOK, P)
```
